# Optimizing a Trainium2 kernel written in Bass

```python
import numpy as np
import jax
import jax.numpy as jnp

def _softmax(x, axis=-1):
    return jax.nn.softmax(x, axis=axis)

def _gelu(x):
    return jax.nn.gelu(x, approximate=True)

def _silu(x):
    return jax.nn.silu(x)

def _sigmoid(x):
    return jax.nn.sigmoid(x)

def _layernorm(x, axis=-1, eps=1e-05):
    m = jnp.mean(x, axis=axis, keepdims=True)
    v = jnp.var(x, axis=axis, keepdims=True)
    return (x - m) / jnp.sqrt(v + eps)

def _scatter_add(tgt, idx, src, axis=0):
    return tgt.at[idx].add(src)

def _segment_sum(src, seg, n):
    return jax.ops.segment_sum(src, seg, n)
kernel_name = 'mk_adaln_attn_ffn_d1_seqx_r4_b85a25'

def setup_inputs(seed: int=0):
    np.random.seed(seed)
    _w = jnp.asarray

    def _rec_inputs():
        import jax
        import jax.numpy as jnp
        _rk = jax.random.key(seed)
        x = -7.109e-05 + 0.9999 * jax.random.normal(jax.random.fold_in(_rk, 1), (64, 64, 512), jnp.float32)
        _lenS = 64 - jax.random.randint(jax.random.fold_in(_rk, 7), (64,), 0, max(1, 64 // 4) + 1, jnp.int32)
        _lenS2 = 64 - jax.random.randint(jax.random.fold_in(_rk, 8), (64,), 0, max(1, 64 // 4) + 1, jnp.int32)
        itok_B_1_198 = jax.random.randint(jax.random.fold_in(_rk, 11), (64,), 1, 199, jnp.int32)
        itok_B_0_6 = jax.random.randint(jax.random.fold_in(_rk, 12), (64,), 0, 7, jnp.int32)
        return (x, itok_B_1_198, itok_B_0_6)
    x, itok_B_1_198, itok_B_0_6 = _rec_inputs()

    def _L0_cond_setup():
        import jax, jax.numpy as jnp
        import numpy as np
        B, C, T = (128, 64, 512)
        S, D = (200, 64)
        key = jax.random.key(seed)
        k1, k2, k3 = jax.random.split(key, 3)
        x = jax.random.normal(k1, (B, C, T), dtype=jnp.float32)
        conditions = jax.random.randint(k2, (B,), 0, S, dtype=jnp.int64)
        weights = jax.random.normal(k3, (S, C, D), dtype=jnp.float32) / jnp.sqrt(jnp.float32(C))
        return {'x': x, 'conditions': conditions, 'weights': weights}
    _L0_cond_all = _L0_cond_setup()
    _L0_cond_in = {k: v for k, v in _L0_cond_all.items() if k in ('weights',)}
    del _L0_cond_all

    def _L0_attn_setup():
        import jax, jax.numpy as jnp
        import numpy as np
        import math
        HIDDEN = 512
        NUM_HEADS = 16
        NUM_KV_HEADS = 8
        HEAD_DIM = HIDDEN // NUM_HEADS
        ROPE_THETA = 1000000.0
        SPARSITY_RATIO = 0.5
        VISION_SPARSITY_RATIO = 0.4
        BATCH = 2
        SEQ = 512

        def rotate_half(x):
            h = x.shape[-1] // 2
            return jnp.concatenate([-x[..., h:], x[..., :h]], axis=-1)
        key = jax.random.key(seed)
        ks = jax.random.split(key, 12)
        s = 1.0 / math.sqrt(HIDDEN)
        return {'hidden_states': jax.random.normal(ks[0], (BATCH, SEQ, HIDDEN), jnp.float32), 'Wq': jax.random.normal(ks[1], (HIDDEN, NUM_HEADS * HEAD_DIM), jnp.float32) * s, 'bq': jax.random.normal(ks[2], (NUM_HEADS * HEAD_DIM,), jnp.float32) * 0.01, 'Wk': jax.random.normal(ks[3], (HIDDEN, NUM_KV_HEADS * HEAD_DIM), jnp.float32) * s, 'bk': jax.random.normal(ks[4], (NUM_KV_HEADS * HEAD_DIM,), jnp.float32) * 0.01, 'Wv': jax.random.normal(ks[5], (HIDDEN, NUM_KV_HEADS * HEAD_DIM), jnp.float32) * s, 'bv': jax.random.normal(ks[6], (NUM_KV_HEADS * HEAD_DIM,), jnp.float32) * 0.01, 'Wo': jax.random.normal(ks[7], (NUM_HEADS * HEAD_DIM, HIDDEN), jnp.float32) * s, 'bo': jax.random.normal(ks[8], (HIDDEN,), jnp.float32) * 0.01, 'Wr': jax.random.normal(ks[9], (HIDDEN, NUM_HEADS), jnp.float32) * s, 'br': jax.random.normal(ks[10], (NUM_HEADS,), jnp.float32) * 0.01}
    _L0_attn_all = _L0_attn_setup()
    _L0_attn_in = {k: v for k, v in _L0_attn_all.items() if k in ('Wq', 'bq', 'Wk', 'bk', 'Wv', 'bv', 'Wo', 'bo', 'Wr', 'br')}
    del _L0_attn_all

    def _L0_cond2_setup():
        import jax, jax.numpy as jnp
        import numpy as np
        B, T, D_IN, D_OUT = (16, 512, 512, 512)
        N_ADAPTERS, RANK = (8, 16)
        key = jax.random.key(seed)
        k_x, k_w, k_a, k_b, k_s, k_idx = jax.random.split(key, 6)
        x = jax.random.normal(k_x, (B, T, D_IN), dtype=jnp.float32)
        W = jax.random.normal(k_w, (D_OUT, D_IN), dtype=jnp.float32) * (1.0 / np.sqrt(D_IN))
        A = jax.random.normal(k_a, (N_ADAPTERS, RANK, D_IN), dtype=jnp.float32) * 0.02
        Bm = jax.random.normal(k_b, (N_ADAPTERS, D_OUT, RANK), dtype=jnp.float32) * 0.02
        scalings = jnp.ones((N_ADAPTERS,), dtype=jnp.float32)
        adapter_idx = jax.random.randint(k_idx, (B,), 0, N_ADAPTERS, dtype=jnp.int32)
        return {'x': x, 'W': W, 'A': A, 'Bm': Bm, 'scalings': scalings, 'adapter_idx': adapter_idx}
    _L0_cond2_all = _L0_cond2_setup()
    _L0_cond2_in = {k: v for k, v in _L0_cond2_all.items() if k in ('W', 'A', 'Bm', 'scalings')}
    del _L0_cond2_all

    def _L0_ffn_setup():
        import jax, jax.numpy as jnp
        import numpy as np
        BLOCK_SIZE = 32
        HIDDEN_SIZE = 512
        MLP_DIM = 4096
        NVFP4_LUT = jnp.array([0.0, 0.5, 1.0, 1.5, 2.0, 3.0, 4.0, 6.0, 0.0, -0.5, -1.0, -1.5, -2.0, -3.0, -4.0, -6.0], dtype=jnp.float32)

        def dequant_nvfp4(W_packed, scales, block=BLOCK_SIZE):
            N = W_packed.shape[0]
            low = W_packed & 15
            high = W_packed >> 4 & 15
            idx = jnp.stack([low, high], axis=-1).reshape(N, -1)
            vals = NVFP4_LUT[idx]
            K = vals.shape[1]
            vals = vals.reshape(N, K // block, block) * scales[:, :, None]
            return vals.reshape(N, K)
        key = jax.random.key(seed)
        ks = jax.random.split(key, 7)
        x = jax.random.normal(ks[0], (4, 32, HIDDEN_SIZE), dtype=jnp.float32)
        gate_W_packed = jax.random.randint(ks[1], (MLP_DIM, HIDDEN_SIZE // 2), 0, 64, dtype=jnp.int32)
        gate_scales = jax.random.uniform(ks[2], (MLP_DIM, HIDDEN_SIZE // BLOCK_SIZE), dtype=jnp.float32) * 0.1 + 0.001
        up_W_packed = jax.random.randint(ks[3], (MLP_DIM, HIDDEN_SIZE // 2), 0, 64, dtype=jnp.int32)
        up_scales = jax.random.uniform(ks[4], (MLP_DIM, HIDDEN_SIZE // BLOCK_SIZE), dtype=jnp.float32) * 0.1 + 0.001
        down_W_packed = jax.random.randint(ks[5], (HIDDEN_SIZE, MLP_DIM // 2), 0, 64, dtype=jnp.int32)
        down_scales = jax.random.uniform(ks[6], (HIDDEN_SIZE, MLP_DIM // BLOCK_SIZE), dtype=jnp.float32) * 0.1 + 0.001
        return {'x': x, 'gate_W_packed': gate_W_packed, 'gate_scales': gate_scales, 'up_W_packed': up_W_packed, 'up_scales': up_scales, 'down_W_packed': down_W_packed, 'down_scales': down_scales}
    _L0_ffn_all = _L0_ffn_setup()
    _L0_ffn_in = {k: v for k, v in _L0_ffn_all.items() if k in ('gate_W_packed', 'gate_scales', 'up_W_packed', 'up_scales', 'down_W_packed', 'down_scales')}
    del _L0_ffn_all
    return {'x': x, 'itok_B_1_198': itok_B_1_198, 'itok_B_0_6': itok_B_0_6, 'L0_cond_weights': _L0_cond_in['weights'], 'L0_attn_Wq': _L0_attn_in['Wq'], 'L0_attn_bq': _L0_attn_in['bq'], 'L0_attn_Wk': _L0_attn_in['Wk'], 'L0_attn_bk': _L0_attn_in['bk'], 'L0_attn_Wv': _L0_attn_in['Wv'], 'L0_attn_bv': _L0_attn_in['bv'], 'L0_attn_Wo': _L0_attn_in['Wo'], 'L0_attn_bo': _L0_attn_in['bo'], 'L0_attn_Wr': _L0_attn_in['Wr'], 'L0_attn_br': _L0_attn_in['br'], 'L0_cond2_W': _L0_cond2_in['W'], 'L0_cond2_A': _L0_cond2_in['A'], 'L0_cond2_Bm': _L0_cond2_in['Bm'], 'L0_cond2_scalings': _L0_cond2_in['scalings'], 'L0_ffn_gate_W_packed': _L0_ffn_in['gate_W_packed'], 'L0_ffn_gate_scales': _L0_ffn_in['gate_scales'], 'L0_ffn_up_W_packed': _L0_ffn_in['up_W_packed'], 'L0_ffn_up_scales': _L0_ffn_in['up_scales'], 'L0_ffn_down_W_packed': _L0_ffn_in['down_W_packed'], 'L0_ffn_down_scales': _L0_ffn_in['down_scales']}

def reference(x, itok_B_1_198, itok_B_0_6, L0_cond_weights, L0_attn_Wq, L0_attn_bq, L0_attn_Wk, L0_attn_bk, L0_attn_Wv, L0_attn_bv, L0_attn_Wo, L0_attn_bo, L0_attn_Wr, L0_attn_br, L0_cond2_W, L0_cond2_A, L0_cond2_Bm, L0_cond2_scalings, L0_ffn_gate_W_packed, L0_ffn_gate_scales, L0_ffn_up_W_packed, L0_ffn_up_scales, L0_ffn_down_W_packed, L0_ffn_down_scales):
    import jax
    import jax.numpy as jnp

    def _L0_cond_ref(x, conditions, weights):
        import jax, jax.numpy as jnp
        import numpy as np
        B, C, T = (128, 64, 512)
        S, D = (200, 64)
        w = weights[conditions]
        return jnp.einsum('bct,bcd->bdt', x, w)

    def _L0_attn_ref(hidden_states, Wq, bq, Wk, bk, Wv, bv, Wo, bo, Wr, br):
        import jax, jax.numpy as jnp
        import numpy as np
        import math
        HIDDEN = 512
        NUM_HEADS = 16
        NUM_KV_HEADS = 8
        HEAD_DIM = HIDDEN // NUM_HEADS
        ROPE_THETA = 1000000.0
        SPARSITY_RATIO = 0.5
        VISION_SPARSITY_RATIO = 0.4
        BATCH = 2
        SEQ = 512

        def rotate_half(x):
            h = x.shape[-1] // 2
            return jnp.concatenate([-x[..., h:], x[..., :h]], axis=-1)
        bsz, q_len, _ = hidden_states.shape
        q = (hidden_states @ Wq + bq).reshape(bsz, q_len, NUM_HEADS, HEAD_DIM).transpose(0, 2, 1, 3)
        k = (hidden_states @ Wk + bk).reshape(bsz, q_len, NUM_KV_HEADS, HEAD_DIM).transpose(0, 2, 1, 3)
        v = (hidden_states @ Wv + bv).reshape(bsz, q_len, NUM_KV_HEADS, HEAD_DIM).transpose(0, 2, 1, 3)
        pos = jnp.arange(q_len, dtype=jnp.float32)
        inv_freq = 1.0 / ROPE_THETA ** (jnp.arange(0, HEAD_DIM, 2, dtype=jnp.float32) / HEAD_DIM)
        freqs = pos[:, None] * inv_freq[None, :]
        emb = jnp.concatenate([freqs, freqs], axis=-1)
        cos = jnp.cos(emb)[None, None, :, :]
        sin = jnp.sin(emb)[None, None, :, :]
        q = q * cos + rotate_half(q) * sin
        k = k * cos + rotate_half(k) * sin
        n_rep = NUM_HEADS // NUM_KV_HEADS
        k = jnp.repeat(k, n_rep, axis=1)
        v = jnp.repeat(v, n_rep, axis=1)
        routing = jax.nn.sigmoid(hidden_states @ Wr + br).transpose(0, 2, 1)
        ratio = VISION_SPARSITY_RATIO if q_len > 128 else SPARSITY_RATIO
        topk = max(1, min(int(q_len * ratio), q_len))
        _, idx = jax.lax.top_k(routing, topk)
        mask = jax.vmap(jax.vmap(lambda i: jnp.zeros((q_len,), bool).at[i].set(True)))(idx)
        scores = jnp.einsum('bhqd,bhkd->bhqk', q, k) / math.sqrt(HEAD_DIM)
        sparse = jnp.where(mask[:, :, None, :], scores, -jnp.inf)
        probs = jax.nn.softmax(sparse.astype(jnp.float32), axis=-1).astype(q.dtype)
        out = jnp.einsum('bhqk,bhkd->bhqd', probs, v)
        out = out.transpose(0, 2, 1, 3).reshape(bsz, q_len, NUM_HEADS * HEAD_DIM)
        return out @ Wo + bo

    def _L0_cond2_ref(x, W, A, Bm, scalings, adapter_idx):
        import jax, jax.numpy as jnp
        import numpy as np
        B, T, D_IN, D_OUT = (16, 512, 512, 512)
        N_ADAPTERS, RANK = (8, 16)
        H = jnp.einsum('btd,od->bto', x, W)
        A_b = A[adapter_idx]
        B_b = Bm[adapter_idx]
        s_b = scalings[adapter_idx]
        xa = jnp.einsum('btd,brd->btr', x, A_b)
        delta = jnp.einsum('btr,bor->bto', xa, B_b)
        delta = jax.lax.stop_gradient(delta * s_b[:, None, None])
        return H + delta

    def _L0_ffn_ref(x, gate_W_packed, gate_scales, up_W_packed, up_scales, down_W_packed, down_scales):
        import jax, jax.numpy as jnp
        import numpy as np
        BLOCK_SIZE = 32
        HIDDEN_SIZE = 512
        MLP_DIM = 4096
        NVFP4_LUT = jnp.array([0.0, 0.5, 1.0, 1.5, 2.0, 3.0, 4.0, 6.0, 0.0, -0.5, -1.0, -1.5, -2.0, -3.0, -4.0, -6.0], dtype=jnp.float32)

        def dequant_nvfp4(W_packed, scales, block=BLOCK_SIZE):
            N = W_packed.shape[0]
            low = W_packed & 15
            high = W_packed >> 4 & 15
            idx = jnp.stack([low, high], axis=-1).reshape(N, -1)
            vals = NVFP4_LUT[idx]
            K = vals.shape[1]
            vals = vals.reshape(N, K // block, block) * scales[:, :, None]
            return vals.reshape(N, K)
        B, S, H = x.shape
        xt = x.reshape(B * S, H)
        Wg = dequant_nvfp4(gate_W_packed, gate_scales)
        Wu = dequant_nvfp4(up_W_packed, up_scales)
        Wd = dequant_nvfp4(down_W_packed, down_scales)
        gate = jnp.einsum('th,nh->tn', xt, Wg)
        up = jnp.einsum('th,nh->tn', xt, Wu)
        gelu = jnp.tanh(0.7978845608028654 * (gate + 0.044715 * gate ** 3)) * gate * 0.5 + gate * 0.5
        inter = gelu * up
        out = jnp.einsum('tn,hn->th', inter, Wd)
        return out.reshape(B, S, H)
    x = x + _L0_attn_ref(_L0_cond_ref(x, itok_B_1_198, L0_cond_weights), L0_attn_Wq, L0_attn_bq, L0_attn_Wk, L0_attn_bk, L0_attn_Wv, L0_attn_bv, L0_attn_Wo, L0_attn_bo, L0_attn_Wr, L0_attn_br)
    x = x + _L0_ffn_ref(_L0_cond2_ref(x, L0_cond2_W, L0_cond2_A, L0_cond2_Bm, L0_cond2_scalings, itok_B_0_6), L0_ffn_gate_W_packed, L0_ffn_gate_scales, L0_ffn_up_W_packed, L0_ffn_up_scales, L0_ffn_down_W_packed, L0_ffn_down_scales)
    return x

_drawn_inputs = setup_inputs


def setup_inputs(seed=0):
    import zlib

    import numpy as np

    out = dict(_drawn_inputs(seed))
    spreads = {'L0_cond2_scalings': (1.0, 0.6)}
    factors = {'L0_attn_bq': 8.0, 'L0_attn_bk': 39.088, 'L0_attn_bv': 5.378, 'L0_attn_bo': 7.645}
    for name, (base, spread) in spreads.items():
        noise = np.random.default_rng([zlib.crc32(name.encode()), seed]).standard_normal(out[name].shape)
        drawn = base * np.exp(spread * noise) if base else spread * noise
        out[name] = jnp.asarray(drawn.astype(out[name].dtype))
    for name, factor in factors.items():
        out[name] = (out[name] * factor).astype(out[name].dtype)
    return out
```

```python
from contextlib import ExitStack

import numpy as np

import concourse.bass as bass
from concourse import mybir

F32 = mybir.dt.float32
F32R = mybir.dt.float32r
I32 = mybir.dt.int32
U32 = mybir.dt.uint32
BF16 = mybir.dt.bfloat16
ALU = mybir.AluOpType
ACT = mybir.ActivationFunctionType
AX_X = mybir.AxisListType.X

P = 128
HEADS, KV_HEADS, HD = 16, 8, 32
ROPE_THETA = 1000000.0
RANK, ADAPTERS = 16, 8
TILE = 512
SIGMOID_ONE = 24 * float(np.log(2.0))
SIGMOID_ZERO = -88.72
PICKED = -1.0e30
MASKED = -1.0e30
GELU_CUBIC = 0.044715
GELU_SCALE = 0.7978845608028654
HI, LO = 0, 1


def split_product(passes):
    return [(HI, HI), (HI, LO), (LO, HI)]


THREE = split_product(3)


def build(nc, a, out):
    B, C, D = a["x"].shape
    NCP = a["gate_packed"].shape[0]
    KC = D // P
    NB = TILE // C
    NP = NB // 2
    NT = B // NB
    GB = 4
    NG = NCP // GB
    NS = 2 * GB
    TOPK = C // 2
    assert D == TILE and C == 64 and NCP >= 2 * GB and NT % 2 == 0 and NT >= 4 and NCP - NT == NT
    ATT_SCALE = HD ** -0.5

    h_scr = nc.dram_tensor("h_scratch", (NT, P, KC, 2, TILE), F32, kind="Internal").ap()
    w_scr = nc.dram_tensor("w_scratch", (NCP, P, 3, 2, 2, 512), F32, kind="Internal").ap()
    z_scr = nc.dram_tensor("z_scratch", (NT, NB, HEADS, C), F32, kind="Internal").ap()
    m_scr = nc.dram_tensor("m_scratch", (NT, NB, HEADS, C), BF16, kind="Internal").ap()

    x_v = a["x"].rearrange("(t q b) c d -> t (b c) q d", q=NP, b=2)
    out_tiles = out.rearrange("(t q b) c d -> t (b c) q d", q=NP, b=2)
    cond_rows = a["cond_weights"].rearrange("s c d -> (s c) d")

    with ExitStack() as ctx:
        def sem(name):
            return ctx.enter_context(nc.semaphore(name))

        def sb_in(stack):
            return lambda name, shape, dt: stack.enter_context(nc.sbuf_tensor(name, shape, dt))

        def ps_in(stack):
            return lambda name, shape, dt: stack.enter_context(nc.psum_tensor(name, shape, dt))

        sb = sb_in(ctx)
        packed = sb("packed", [P, 3, 512], I32)
        scales = sb("scales", [P, 3, 512], F32)
        magnitude = sb("magnitude", [P, 512], I32)
        signed_scale = sb("signed_scale", [P, 2, 512], I32)
        lut_line = sb("lut_line", [P, 512], F32)
        lut_v = sb("lut_v", [P, 2, 512], F32)
        w_parts = sb("w_parts", [P, 2, 2, 512], F32R)

        with ExitStack() as token_stage:
            sb = sb_in(token_stage)
            ps = ps_in(token_stage)
            wq = sb("wq", [P, 2, KC, 512], F32R)
            wk = sb("wk", [P, 2, KC, 256], F32R)
            wv = sb("wv", [P, 2, KC, 256], F32R)
            wo = sb("wo", [P, 2, KC, 512], F32R)
            w2 = sb("w2", [P, 2, KC, 512], F32R)
            wr = sb("wr", [P, 2, KC, HEADS], F32R)
            wa = sb("wa", [P, 2, KC, P], F32R)
            wb = sb("wb", [P, 2, 512], F32R)
            bq = sb("bq", [P, 4], F32)
            bk = sb("bk", [P, 2], F32)
            bv = sb("bv", [P, 256], F32)
            bo = sb("bo", [P, 512], F32)
            br = sb("br", [HEADS, 1], F32)
            cos = sb("cos", [P, C], F32)
            sin = sb("sin", [P, C], F32)
            identity = sb("identity", [P, P], F32)
            pair_rows = sb("pair_rows", [NB, NP, P], BF16)
            columns = sb("columns", [P, 2], F32)
            adapter_of = sb("adapter_of", [P, B], I32)
            adapter_scale = sb("adapter_scale", [P, 1], F32)
            adapter_mask = sb("adapter_mask", [P, B], F32)
            cond_of = sb("cond_of", [P, B // 2], I32)
            cond_row = sb("cond_row", [P, B // 2], U32)
            mix = sb("mix", [P, B // 2, C], F32)
            mix_tile = sb("mix_tile", [P, 2, NP, 2, C], F32)
            x_in = sb("x_in", [P, 2, NP, D], F32)
            hs = sb("hs", [P, 2, KC, TILE], F32R)
            z_sb = sb("z_sb", [HEADS, TILE], F32)
            z_rows = sb("z_rows", [P, C], F32)
            rank = sb("rank", [P, C], F32)
            top8 = sb("top8", [P, 8], F32)
            key_bias = sb("key_bias", [P, C], BF16)
            bias_rows = sb("bias_rows", [NB, HEADS * C], BF16)
            rope_in = sb("rope_in", [P, 2, TILE], F32)
            rope_sin = sb("rope_sin", [P, 2, TILE], F32)
            v_diag = sb("v_diag", [P, 2, 2, KV_HEADS, 2 * HD], F32)
            probs = sb("probs", [P, 2, HEADS, C], F32)
            row_max = sb("row_max", [P, 2, HEADS], F32)
            row_sum = sb("row_sum", [P, 2, HEADS], F32)
            row_inv = sb("row_inv", [P, 2, HEADS], F32)
            heads_out = sb("heads_out", [P, 2, HEADS, HD], F32)
            attnT = sb("attnT", [P, 2, KC, P], F32R)
            x1T = hs
            with ExitStack() as attention_part:
                sb = sb_in(attention_part)
                qT = sb("qT", [P, 4, TILE], F32)
                kT = sb("kT", [P, 2, TILE], F32)
                probsT = sb("probsT", [P, KV_HEADS, P], F32)
            sb = sb_in(token_stage)
            h_out = sb("h_out", [P, 2, 2, TILE], F32R)
            xa = sb("xa", [P, TILE], F32)
            xa_parts = sb("xa_parts", [P, 2, TILE], F32R)
            sb("tail_pad", [P, 512], F32)
            proj = [ps(f"proj{i}", [P, 512], F32) for i in range(2)]
            scores = ps("scores", [P, 2, HEADS // 2, C], F32)
            pT = ps("pT", [P, KV_HEADS, P], F32)
            pv = ps("pv", [P, KV_HEADS, 2 * HD], F32)
            turn = ps("turn", [P, KC, P], F32)

        with ExitStack() as ffn_stage:
            sb = sb_in(ffn_stage)
            ps = ps_in(ffn_stage)
            w_slot = [sb(f"w_slot{k}", [P, 3, 2, 2, 512], F32R) for k in range(GB)]
            h_in = [sb(f"h_in{k}", [P, KC, 2, TILE], F32R) for k in range(2)]
            acc = [sb(f"acc{k}", [P, NP, D], F32) for k in range(2)]
            gate_sq = sb("gate_sq", [P, TILE], F32)
            gate_in = sb("gate_in", [P, TILE], F32)
            gate_tanh = sb("gate_tanh", [P, TILE], F32)
            gate_val = sb("gate_val", [P, TILE], F32)
            inter = sb("inter", [P, TILE], F32)
            inter_parts = sb("inter_parts", [P, 2, 2, TILE], F32R)
            down = [ps(f"down{i}", [P, D], F32) for i in range(NP)]
            gate = [ps(f"gate{i}", [P, TILE], F32) for i in range(2)]
            up = [ps(f"up{i}", [P, TILE], F32) for i in range(2)]

        index_ld = sem("index_ld")
        const_ld = sem("const_ld")
        const_made = sem("const_made")
        cond_row_ready = sem("cond_row_ready")
        gather_first, gather_rest = sem("gather_first"), sem("gather_rest")
        raw_ld = [sem("raw_ld0"), sem("raw_ld1")]
        raw_hi, raw_lo = sem("raw_hi"), sem("raw_lo")
        mix_cleared, mix_ready = sem("mix_cleared"), sem("mix_ready")
        score_step = sem("score_step")
        x_ld = [sem("x_ld0"), sem("x_ld1")]
        proj_full = [sem("proj_full0"), sem("proj_full1")]
        proj_free = [sem("proj_free0"), sem("proj_free1")]
        hs_hi = sem("hs_hi")
        z_stored, z_ld = sem("z_stored"), sem("z_ld")
        topk_step, bias_ready, bias_stored, bias_ld = sem("topk_step"), sem("bias_ready"), sem("bias_stored"), sem("bias_ld")
        rope_turned, rope_parts, rope_done = sem("rope_turned"), sem("rope_parts"), sem("rope_done")
        scores_max, scores_used = sem("scores_max"), sem("scores_used")
        exp_done, sum_step = sem("exp_done"), sem("sum_step")
        pT_full, pT_used = sem("pT_full"), sem("pT_used")
        pv_full, pv_used = sem("pv_full"), sem("pv_used")
        turn_full, turn_hi, turn_used = sem("turn_full"), sem("turn_hi"), sem("turn_used")
        residual_ready, x1_stored = sem("residual_ready"), sem("x1_stored")
        xa_hi, xa_lo = sem("xa_hi"), sem("xa_lo")
        h_hi = sem("h_hi")
        h_stored = [sem("h_stored0"), sem("h_stored1")]
        packed_ld = [sem(f"packed_ld{m}") for m in range(3)]
        dq_step, w_used, w_step = sem("dq_step"), sem("w_used"), sem("w_step")
        w_stored = [sem("w_stored0"), sem("w_stored1")]
        pool_passed = sem("pool_passed")
        dve_passed = sem("dve_passed")
        sp_passed = sem("sp_passed")
        slot_ld = [sem(f"slot_ld{k}") for k in range(GB)]
        h_ld = [sem("h_ld0"), sem("h_ld1")]
        acc_ld = [sem("acc_ld0"), sem("acc_ld1")]
        acc_stored = [sem("acc_stored0"), sem("acc_stored1")]
        gate_full = [sem("gate_full0"), sem("gate_full1")]
        up_full = [sem("up_full0"), sem("up_full1")]
        down_done, down_full, acc_added = sem("down_done"), sem("down_full"), sem("acc_added")
        sq_done, gin_done, tanh_done, gval_done = sem("sq_done"), sem("gin_done"), sem("tanh_done"), sem("gval_done")
        inter_done, inter_hi, inter_ready = sem("inter_done"), sem("inter_hi"), sem("inter_ready")

        USES = ["hs0", "hs1", "hs2", "hs3", "z", "k0", "k1", "q0", "q1", "q2", "q3",
                "v0", "v1", "v2", "o0", "v3", "o1", "o2", "o3", "xa", "h0", "h1", "h2", "h3"]
        TURNS = ["o0", "o1", "x0", "o2", "x1", "o3", "x2", "x3"]
        SLOTS = NP + 3

        PRIMED = 1

        def use(name):
            n = USES.index(name)
            return n % 2, n // 2

        def full(t, name):
            return t * (len(USES) // 2) + use(name)[1] + 1

        def full_wait(eng, t, name):
            eng.wait_ge(proj_full[use(name)[0]], full(t, name))
            return proj[use(name)[0]]

        def evacuated(eng, t, name):
            eng.wait_ge(proj_free[use(name)[0]], full(t, name) + PRIMED)

        RAW = [("wk", wk, 256), ("wq", wq, 512), ("wr", wr, HEADS), ("wv", wv, 256),
               ("wo", wo, 512), ("w2", w2, 512), ("wa", wa, P), ("wb", wb, None)]
        N_CONST = 11

        def raw_views(j):
            _, parts, cols = RAW[j]
            stage = (probs[:].rearrange("p a h c -> p (a h c)").rearrange("p (k n) -> p k n", k=KC), qT[:])[j % 2]
            if cols is None:
                return stage[:, 0, :], parts[:, HI, :], parts[:, LO, :]
            return stage[:, :, 0:cols], parts[:, HI], parts[:, LO]

        block = ctx.enter_context(nc.Block())

        @block.sync
        def _(sp):
            for q in h_stored:
                sp.sem_inc(q, PRIMED)
            def passed():
                sp.sem_inc(sp_passed, 1)

            sp.dma_start(cond_of[0:C, :], a["cond_index"][0:1, :].to_broadcast([C, B // 2])).then_inc(index_ld, 16)
            sp.dma_start(cond_of[C:P, :], a["cond_index"][1:2, :].to_broadcast([C, B // 2])).then_inc(index_ld, 16)
            sp.dma_start(columns[:], a["columns"]).then_inc(index_ld, 16)
            sp.dma_start(x_in[:, 0], x_v[0]).then_inc(x_ld[0], 16)
            for j, (name, parts, cols) in enumerate(RAW[:2]):
                sp.dma_start(raw_views(j)[0], a[name] if cols is None else a[name].rearrange("(k p) n -> p k n", p=P)).then_inc(raw_ld[j % 2], 16)
            for dst, src in ((bq, a["bq"]), (bk, a["bk"]), (cos, a["cos"]), (sin, a["sin"]),
                             (identity, a["identity"]), (rope_in[0:NB, 0, :].rearrange("b (q p) -> b q p", p=P), a["pair_rows"]), (br, a["br"])):
                sp.dma_start(dst[:], src).then_inc(const_ld, 16)
            sp.dma_start(bv[:], a["bv"].to_broadcast([P, 256])).then_inc(const_ld, 16)
            sp.dma_start(bo[:], a["bo"].to_broadcast([P, 512])).then_inc(const_ld, 16)
            sp.dma_start(adapter_of[:], a["adapter_index"].to_broadcast([P, B])).then_inc(const_ld, 16)
            sp.dma_start(adapter_scale[:], a["adapter_scales"]).then_inc(const_ld, 16)
            sp.dma_start(x_in[:, 1], x_v[1]).then_inc(x_ld[1], 16)
            for j, (name, parts, cols) in enumerate(RAW):
                if j >= 2:
                    sp.wait_ge(raw_lo, j - 1)
                    sp.dma_start(raw_views(j)[0], a[name] if cols is None else a[name].rearrange("(k p) n -> p k n", p=P)).then_inc(raw_ld[j % 2], 16)

            def tile(tt, par, last):
                t = tt * 2 + par
                evacuated(sp, t, "z")
                passed()
                sp.dma_start(z_scr[t].rearrange("b h c -> h b c"), z_sb[:].rearrange("h (b c) -> h b c", c=C)).then_inc(z_stored, 16)
                sp.wait_ge(z_stored, (t + 1) * 16)
                passed()
                sp.dma_start(z_rows[:], z_scr[t].rearrange("b h c -> (b h) c")).then_inc(z_ld, 16)
                sp.wait_ge(bias_ready, t + 1)
                passed()
                sp.dma_start(m_scr[t].rearrange("b h c -> (b h) c"), key_bias[:]).then_inc(bias_stored, 16)
                sp.wait_ge(bias_stored, (t + 1) * 16)
                passed()
                sp.dma_start(bias_rows[:], m_scr[t].rearrange("b h c -> b (h c)")).then_inc(bias_ld, 16)
                evacuated(sp, t, "o2")
                passed()
                evacuated(sp, t, "o3")
                passed()
                sp.dma_start(out_tiles[t], x_in[:, par]).then_inc(x1_stored, 16)
                if not last:
                    sp.wait_ge(x1_stored, (t + 1) * 16)
                    passed()
                    sp.wait_ge(turn_full, (t + 1) * 8)
                    passed()
                    sp.dma_start(x_in[:, par], x_v[t + 2]).then_inc(x_ld[par], 16)
                for n in range(KC):
                    evacuated(sp, t, f"h{n}")
                    passed()
                    sp.dma_start(h_scr[t, :, n], h_out[:, n % 2].bitcast(F32)).then_inc(h_stored[n % 2], 16)

            with sp.Fori(0, NT // 2 - 1) as tt:
                tile(tt, 0, False)
                tile(tt, 1, False)
            tile(NT // 2 - 1, 0, True)
            tile(NT // 2 - 1, 1, True)

            for q in h_stored:
                sp.wait_ge(q, NT * (KC // 2) * 16 + PRIMED)
            sp.wait_ge(x1_stored, NT * 16)

            def load_slot(g, k):
                sp.dma_start(w_slot[k][:].bitcast(F32), w_scr[g * GB + k]).then_inc(slot_ld[k], 16)

            def load_tile(s, par):
                sp.dma_start(h_in[par][:].bitcast(F32), h_scr[s]).then_inc(h_ld[par], 16)

            def load_acc(s, par):
                sp.dma_start(acc[par][:], out_tiles[s]).then_inc(acc_ld[par], 16)

            def weights_stored(blocks):
                for q in w_stored:
                    sp.wait_ge(q, blocks * 48)

            load_tile(0, 0)
            weights_stored(GB)
            for k in range(GB):
                load_slot(0, k)
            load_acc(0, 0)
            load_tile(1, 1)
            load_acc(1, 1)

            def store(i, s, par):
                sp.wait_ge(acc_added, (i + 1) * NP)
                passed()
                sp.dma_start(out_tiles[s], acc[par][:]).then_inc(acc_stored[par], 16)

            def step(pair, i, s_before, s_next):
                sp.wait_ge(down_done, i * (NS - 1) - 1)
                passed()
                load_tile(s_next, 1)
                store(i - 1, s_before, 1)
                sp.wait_ge(acc_stored[1], pair * 16)
                passed()
                load_acc(s_next, 1)

            NPAIR = NT // 2

            def pair_body(g, p, first=False, last_of_group=False, very_last=False):
                pair = g * NPAIR + p
                i0 = pair * 2
                s0 = p * 2
                wrap_before = (NT - 1) if (isinstance(p, int) and p == 0) else s0 - 1
                if not first:
                    step(pair, i0, wrap_before, s0 + 1)
                i1 = i0 + 1
                s_next = 0 if last_of_group else s0 + 2
                if very_last:
                    store(i1 - 1, s0, 0)
                    return
                sp.wait_ge(down_done, i1 * (NS - 1) - 1)
                passed()
                load_tile(s_next, 0)
                if last_of_group:
                    weights_stored_reg((g + 2) * GB)
                    for k in range(GB):
                        if k == GB - 1:
                            store(i1 - 1, s0, 0)
                        if k < GB - 1:
                            sp.wait_ge(down_done, i1 * (NS - 1) + 2 * k + 2)
                        else:
                            sp.wait_ge(down_full, (i1 + 1) * NP)
                        passed()
                        load_slot(g + 1, k)
                else:
                    store(i1 - 1, s0, 0)
                sp.wait_ge(acc_stored[0], (pair + 1) * 16)
                passed()
                load_acc(s_next, 0)

            def weights_stored_reg(blocks):
                for q in w_stored:
                    sp.wait_ge(q, blocks * 48)
                    passed()

            def group(g, last_group):
                if isinstance(g, int) and g == 0:
                    pair_body(0, 0, first=True)
                else:
                    pair_body(g, 0)
                if NPAIR > 2:
                    with sp.Fori(1, NPAIR - 1) as p:
                        pair_body(g, p)
                pair_body(g, NPAIR - 1, last_of_group=True, very_last=last_group)

            group(0, NG == 1)
            if NG > 2:
                with sp.Fori(1, NG - 1) as g:
                    group(g, False)
            group(NG - 1, True)
            i_last = NG * NT - 1
            sp.wait_ge(acc_added, (i_last + 1) * NP)
            sp.dma_start(out_tiles[NT - 1], acc[1][:]).then_inc(acc_stored[1], 16)
            sp.wait_ge(acc_stored[0], NG * NPAIR * 16)
            sp.wait_ge(acc_stored[1], NG * NPAIR * 16)

        @block.gpsimd
        def _(pool):
            pool.sem_inc(w_step, PRIMED)

            def passed():
                pool.sem_inc(pool_passed, 1)

            def load_packed(c, m):
                name = ("gate", "up", "down")[m]
                pool.dma_start(packed[:, m, :], a[name + "_packed"][c]).then_inc(packed_ld[m], 16)
                if m < 2:
                    for k in range(2):
                        pool.dma_start(scales[:, m, k * 256:(k + 1) * 256],
                                       a[name + "_scales"][c, 8 * k:8 * k + 8, :].unsqueeze(1).to_broadcast([8, 16, 256])).then_inc(packed_ld[m], 16)
                else:
                    pool.dma_start(scales[:, m, :], a[name + "_scales"][c].unsqueeze(1).to_broadcast([8, 16, 512])).then_inc(packed_ld[m], 16)

            pool.wait_ge(cond_row_ready, 1)
            for q in range(B // 2):
                pool.indirect_dma_start(mix[:, q, :], None, cond_rows, bass.IndirectOffsetOnAxis(ap=cond_row[:, q:q + 1], axis=0)) \
                    .then_inc(gather_first if q < NP else gather_rest, 16)
            for m in range(3):
                load_packed(0, m)

            def weight_block(c, k, last):
                m, nib = k // 2, k % 2
                par = k % 2
                pool.wait_ge(dq_step, c * 36 + 6 * k + 6)
                pool.tensor_tensor(lut_v[:, par, :], lut_v[:, par, :], signed_scale[:, par, :].bitcast(F32), ALU.mult).then_inc(w_used, 1)
                if nib == 1 and not last:
                    load_packed(c + 1, m)
                if k >= 2:
                    pool.wait_ge(w_stored[par], (c * 3 + m) * 16)
                    passed()
                pool.wait_ge(w_used, c * 6 + k + 1)
                passed()
                pool.tensor_copy(w_parts[:, par, HI, :], lut_v[:, par, :]).then_inc(w_step, 1)
                pool.wait_ge(w_step, c * 12 + 2 * k + 1 + PRIMED)
                pool.tensor_tensor(w_parts[:, par, LO, :], lut_v[:, par, :], w_parts[:, par, HI, :].bitcast(F32), ALU.subtract).then_inc(w_step, 1)
                pool.wait_ge(w_step, c * 12 + 2 * k + 2 + PRIMED)
                passed()
                pool.dma_start(w_scr[c, :, m, nib], w_parts[:, par].bitcast(F32)).then_inc(w_stored[par], 16)
                if k == 5:
                    for q in w_stored:
                        pool.wait_ge(q, (c + 1) * 48)
                        passed()

            def tile(tt, par):
                t = tt * 2 + par
                for c in range(6):
                    pool.wait_ge(rope_turned, t * 6 + c + 1)
                    v = rope_in[:, c % 2, :].rearrange("p (b c) -> p b c", c=C)
                    pool.tensor_tensor(v, v,
                                       cos[:].unsqueeze(1).to_broadcast([P, NB, C]), ALU.mult)
                    w = rope_sin[:, c % 2, :].rearrange("p (b c) -> p b c", c=C)
                    pool.tensor_tensor(w, w, sin[:].unsqueeze(1).to_broadcast([P, NB, C]), ALU.mult).then_inc(rope_parts, 1)
                for q in range(NP):
                    ins = pool.tensor_tensor(x_in[:, par, q, :], x_in[:, par, q, :], bo[:], ALU.add)
                ins.then_inc(residual_ready, 1)
                for k in range(6):
                    weight_block(t, k, False)

            pool.wait_ge(const_ld, N_CONST * 16)
            with pool.Fori(0, NT // 2) as tt:
                tile(tt, 0)
                tile(tt, 1)
            with pool.Fori(NT, NCP - 1) as c:
                for k in range(6):
                    weight_block(c, k, False)
            for k in range(6):
                weight_block(NCP - 1, k, True)
            for q in w_stored:
                pool.wait_ge(q, NCP * 48)

        @block.tensor
        def _(pe):
            def ready(t, name):
                par, n = use(name)
                pe.wait_ge(proj_free[par], t * (len(USES) // 2) + n + PRIMED)
                return proj[par], proj_full[par]

            def products(out_ap, pairs):
                for n, (lhsT, rhs) in enumerate(pairs):
                    ins = pe.matmul(out_ap, lhsT, rhs, start=(n == 0), stop=(n == len(pairs) - 1))
                return ins

            def tile(tt, par):
                t = tt * 2 + par
                pe.wait_ge(x_ld[par], (tt + 1) * 16)
                pe.wait_ge(mix_ready, t * 2 + 2)
                for c in range(KC):
                    bank, done = ready(t, f"hs{c}")
                    for q in range(NP):
                        ins = pe.matmul(bank[:, q * P:(q + 1) * P], x_in[:, par, q, c * P:(c + 1) * P],
                                        mix_tile[:, par, q].rearrange("p b c -> p (b c)"), start=True, stop=True)
                    ins.then_inc(done, 1)
                bank, done = ready(t, "z")
                evacuated(pe, t, "hs2")
                evacuated(pe, t, "hs3")
                products(bank[0:HEADS, :], [(wr[:, i, c, :], hs[:, j, c, :]) for c in range(KC) for i, j in THREE]).then_inc(done, 1)
                for n in range(2):
                    bank, done = ready(t, f"k{n}")
                    products(bank[:], [(wk[:, i, c, n * P:(n + 1) * P], hs[:, j, c, :]) for c in range(KC) for i, j in THREE]).then_inc(done, 1)
                for n in range(4):
                    bank, done = ready(t, f"q{n}")
                    products(bank[:], [(wq[:, i, c, n * P:(n + 1) * P], hs[:, j, c, :]) for c in range(KC) for i, j in THREE]).then_inc(done, 1)

                def value(q):
                    bank, done = ready(t, f"v{q}")
                    products(bank[:, 0:256], [(hs[:, i, c, q * P:(q + 1) * P], wv[:, j, c, :]) for c in range(KC) for i, j in THREE]).then_inc(done, 1)

                def score(q):
                    if q == 0:
                        pe.wait_ge(bias_ld, (t + 1) * 16)
                        pe.wait_ge(rope_done, (t + 1) * 6)
                    pe.wait_ge(scores_used, t * NP + q + PRIMED)
                    for gc in range(2):
                        pe.matmul(scores[:, gc].rearrange("p h c -> p (h c)"), pair_rows[:, q, :], bias_rows[:, gc * 512:(gc + 1) * 512],
                                  start=True, stop=False, skip_group_check=True)
                    for i in range(4):
                        for gc in range(2):
                            if i > 0:
                                pe.wait_ge(score_step, (t * NP + q) * 8 + 2 * (i - 1) + gc + 1)
                            for r in range(2):
                                for b in range(2):
                                    cols = slice(q * P + b * C, q * P + (b + 1) * C)
                                    ins = pe.matmul(scores[b * C:(b + 1) * C, gc, 2 * i + r, :],
                                                    qT[32 * i:32 * i + 32, 2 * gc + r, cols],
                                                    kT[32 * i:32 * i + 32, gc, cols],
                                                    start=False, stop=True, skip_group_check=True,
                                                    tile_position=(32 * i, b * C))
                            ins.then_inc(score_step, 1)

                def turn_probs(q):
                    pe.wait_ge(exp_done, t * NP + q + 1)
                    pe.wait_ge(pT_used, t * NP + q + PRIMED)
                    for g in range(KV_HEADS):
                        ins = pe.transpose(pT[:, g, :], probs[:, q % 2, 2 * g:2 * g + 2, :].rearrange("p h c -> p (h c)"), identity[:])
                    ins.then_inc(pT_full, 1)

                def attend(q):
                    pe.wait_ge(pT_used, t * NP + q + 1 + PRIMED)
                    evacuated(pe, t, f"v{q}")
                    pe.wait_ge(pv_used, t * NP + q + PRIMED)
                    for b in range(2):
                        for g in range(KV_HEADS):
                            ins = pe.matmul(pv[b * C:(b + 1) * C, g, :], probsT[:, g, b * C:(b + 1) * C],
                                            v_diag[:, q % 2, b, g, :], start=True, stop=True, tile_position=(0, b * C))
                    ins.then_inc(pv_full, 1)

                def turn_block(name, src):
                    pe.wait_ge(turn_used, t * 8 + TURNS.index(name) + PRIMED)
                    for c in range(KC):
                        ins = pe.transpose(turn[:, c, :], src[:, c * P:(c + 1) * P], identity[:])
                    ins.then_inc(turn_full, 1)

                def out_proj(q):
                    bank, done = ready(t, f"o{q}")
                    pe.wait_ge(turn_used, t * 8 + TURNS.index(f"o{q}") + 1 + PRIMED)
                    products(bank[:], [(attnT[:, i, c, :], wo[:, j, c, :]) for c in range(KC) for i, j in THREE]).then_inc(done, 1)

                for slot in range(SLOTS):
                    if slot < NP:
                        value(slot)
                        score(slot)
                    if 1 <= slot <= NP:
                        turn_probs(slot - 1)
                        attend(slot - 1)
                    if 2 <= slot <= NP + 1:
                        q = slot - 2
                        pe.wait_ge(pv_used, t * NP + q + 1 + PRIMED)
                        turn_block(f"o{q}", heads_out[:, q % 2].rearrange("p h d -> p (h d)"))
                        out_proj(q)
                    if slot >= 3:
                        q = slot - 3
                        evacuated(pe, t, f"o{q}")
                        turn_block(f"x{q}", x_in[:, par, q, :])

                bank, done = ready(t, "xa")
                pe.wait_ge(turn_used, (t + 1) * 8 + PRIMED)
                products(bank[:], [(wa[:, i, c, :], x1T[:, j, c, :]) for c in range(KC) for i, j in THREE]).then_inc(done, 1)
                for n in range(KC):
                    bank, done = ready(t, f"h{n}")
                    cols = slice(n * P, (n + 1) * P)
                    pairs = [(w2[:, i, c, cols], x1T[:, j, c, :]) for c in range(KC) for i, j in THREE]
                    for m, (lhsT, rhs) in enumerate(pairs):
                        pe.matmul(bank[:], lhsT, rhs, start=(m == 0), stop=False)
                    if n == 0:
                        pe.wait_ge(xa_lo, t + 1)
                    for m, (i, j) in enumerate(THREE):
                        ins = pe.matmul(bank[:], wb[:, i, cols], xa_parts[:, j, :], start=False, stop=(m == 2))
                    ins.then_inc(done, 1)

            pe.wait_ge(const_made, 1)
            pe.wait_ge(raw_lo, len(RAW))
            with pe.Fori(0, NT // 2) as tt:
                tile(tt, 0)
                tile(tt, 1)

            def gate_up(i, g, pair, j, par, first):
                k, nib_n = j // 2, j % 2
                if j == 0:
                    pe.wait_ge(h_ld[par], (pair + 1) * 16)
                if j % 2 == 0:
                    pe.wait_ge(slot_ld[k], (g + 1) * 16)
                if j >= 2 or not first:
                    pe.wait_ge(inter_done, i * NS + j - 1)
                for m, bank, done in ((0, gate, gate_full), (1, up, up_full)):
                    pairs = [(w_slot[k][:, m, nib, u, c * 256 + nib_n * P:c * 256 + (nib_n + 1) * P], h_in[par][:, 2 * c + nib, v, :])
                             for c in range(2) for nib in range(2) for u, v in THREE]
                    products(bank[j % 2][:], pairs).then_inc(done[j % 2], 1)

            def down_step(i, j, first=False):
                k, nib_n = j // 2, j % 2
                pe.wait_ge(inter_ready, i * NS + j + 1)
                for tc in range(NP):
                    if j == 0 and not first:
                        pe.wait_ge(acc_added, (i - 1) * NP + tc + 1)
                    for m, (u, v) in enumerate(THREE):
                        ins = pe.matmul(down[tc][:], inter_parts[:, j % 2, u, tc * P:(tc + 1) * P], w_slot[k][:, 2, nib_n, v, :],
                                        start=(j == 0 and m == 0), stop=(j == NS - 1 and m == 2))
                    if j == NS - 1:
                        ins.then_inc(down_full, 1)
                if j < NS - 1:
                    ins.then_inc(down_done, 1)

            def ffn_tile(g, pair, par, first=False):
                i = pair * 2 + par
                for j in range(NS):
                    gate_up(i, g, pair, j, par, first)
                    if j >= 2:
                        down_step(i, j - 2, first)
                    elif not first:
                        down_step(i - 1, NS - 2 + j)

            NPAIR = NT // 2
            ffn_tile(0, 0, 0, first=True)
            ffn_tile(0, 0, 1)
            with pe.Fori(1, NPAIR) as p:
                ffn_tile(0, p, 0)
                ffn_tile(0, p, 1)
            with pe.Fori(1, NG) as g:
                with pe.Fori(0, NPAIR) as p:
                    ffn_tile(g, g * NPAIR + p, 0)
                    ffn_tile(g, g * NPAIR + p, 1)
            for j in (NS - 2, NS - 1):
                down_step(NG * NT - 1, j)

        @block.scalar
        def _(act):
            act.sem_inc(pT_used, PRIMED)
            for j in range(len(RAW)):
                stage, hi, lo = raw_views(j)
                act.wait_ge(raw_ld[j % 2], (j // 2 + 1) * 16)
                act.activation(hi, stage, ACT.Copy).then_inc(raw_hi, 1)
            act.wait_ge(const_ld, N_CONST * 16)
            act.wait_ge(mix_cleared, 1)

            def tile(tt, par):
                t = tt * 2 + par
                if par == 0:
                    act.wait_ge(gather_first, NP * 16)
                else:
                    act.wait_ge(gather_rest, (B // 2 - NP) * 16)
                for b in range(2):
                    rows = slice(b * C, (b + 1) * C)
                    act.activation(mix_tile[rows, par, :, b, :], mix[rows, bass.ds(t * NP, NP), :], ACT.Copy).then_inc(mix_ready, 1)
                for c in range(KC):
                    bank = full_wait(act, t, f"hs{c}")
                    act.activation(hs[:, HI, c, :], bank[:], ACT.Copy).then_inc(hs_hi, 1)
                bank = full_wait(act, t, "z")
                act.activation(z_sb[:], bank[0:HEADS, :], ACT.Identity, bias=br[:, 0:1]).then_inc(proj_free[use("z")[0]], 1)
                for c, name in enumerate(("k0", "k1", "q0", "q1", "q2", "q3")):
                    bank = full_wait(act, t, name)
                    bias = bk[:, c:c + 1] if c < 2 else bq[:, c - 2:c - 1]
                    if c >= 2:
                        act.wait_ge(rope_done, t * 6 + c - 1)
                    act.activation(rope_in[:, c % 2, :], bank[:], ACT.Identity, bias=bias).then_inc(proj_free[use(name)[0]], 1)
                for slot in range(SLOTS):
                    if 1 <= slot <= NP:
                        q = slot - 1
                        act.wait_ge(pT_full, t * NP + q + 1)
                        act.activation(probsT[:], pT[:], ACT.Copy).then_inc(pT_used, 1)
                    if slot < NP:
                        act.wait_ge(scores_used, t * NP + slot + 1 + PRIMED)
                        pr = probs[:, slot % 2]
                        act.activation(pr, pr, ACT.Exp, scale=ATT_SCALE).then_inc(exp_done, 1)
                    if 2 <= slot <= NP + 1:
                        n = TURNS.index(f"o{slot - 2}")
                        act.wait_ge(turn_full, t * 8 + n + 1)
                        act.activation(attnT[:, HI], turn[:], ACT.Copy).then_inc(turn_hi, 1)
                    if slot >= 3:
                        q = slot - 3
                        n = TURNS.index(f"x{q}")
                        act.wait_ge(turn_full, t * 8 + n + 1)
                        act.activation(x1T[:, HI, :, q * P:(q + 1) * P], turn[:], ACT.Copy).then_inc(turn_hi, 1)
                evacuated(act, t, "xa")
                act.activation(xa_parts[:, HI, :], xa[:], ACT.Copy).then_inc(xa_hi, 1)
                for n in range(KC):
                    act.wait_ge(h_stored[n % 2], (t * (KC // 2) + n // 2) * 16 + PRIMED)
                    bank = full_wait(act, t, f"h{n}")
                    act.activation(h_out[:, n % 2, HI, :], bank[:], ACT.Copy).then_inc(h_hi, 1)

            with act.Fori(0, NT // 2) as tt:
                tile(tt, 0)
                tile(tt, 1)

            def ffn_tile(i, first=False):
                for j in range(NS):
                    b = j % 2
                    n = i * (NS // 2) + j // 2
                    act.wait_ge(gate_full[b], n + 1)
                    act.activation(gate_sq[:], gate[b][:], ACT.Square).then_inc(sq_done, 1)
                    act.wait_ge(gin_done, i * NS + j + 1)
                    act.activation(gate_tanh[:], gate_in[:], ACT.Tanh, scale=GELU_SCALE * GELU_CUBIC).then_inc(tanh_done, 1)
                    if not (first and j < 2):
                        if j == 1:
                            act.wait_ge(down_full, i * NP)
                        else:
                            act.wait_ge(down_done, i * (NS - 1) + max(j - 1, 0))
                    act.wait_ge(inter_done, i * NS + j + 1)
                    act.activation(inter_parts[:, b, HI, :], inter[:], ACT.Copy).then_inc(inter_hi, 1)

            ffn_tile(0, first=True)
            with act.Fori(1, NG * NT) as i:
                ffn_tile(i)

        @block.vector
        def _(dve):
            for q in (*proj_free, scores_used, pv_used, turn_used):
                dve.sem_inc(q, PRIMED)

            def passed():
                dve.sem_inc(dve_passed, 1)

            dve.wait_ge(index_ld, 48)
            dve.tensor_scalar(cond_row[:], cond_of[:], float(C), columns[:, 0:1], ALU.mult, ALU.add).then_inc(cond_row_ready, 1)
            dve.memset(v_diag[:], 0.0)
            dve.memset(mix_tile[:], 0.0).then_inc(mix_cleared, 1)
            for j in range(len(RAW)):
                stage, hi, lo = raw_views(j)
                dve.wait_ge(raw_hi, j + 1)
                dve.tensor_tensor(lo, stage, hi.bitcast(F32), ALU.subtract).then_inc(raw_lo, 1)
            dve.wait_ge(const_ld, N_CONST * 16)
            dve.tensor_copy(pair_rows[:], rope_in[0:NB, 0, :].rearrange("b (q p) -> b q p", p=P))
            dve.tensor_scalar(adapter_mask[:], adapter_of[:], columns[:, 1:2], adapter_scale[:, 0:1],
                              ALU.is_equal, ALU.mult).then_inc(const_made, 1)

            def dequantise(c, k):
                m, nib = k // 2, k % 2
                base = c * 36 + 6 * k
                if nib == 0:
                    dve.wait_ge(packed_ld[m], (c + 1) * (48 if m < 2 else 32))
                if k >= 2:
                    dve.wait_ge(w_step, c * 12 + 2 * k - 2 + PRIMED)
                elif k == 0:
                    dve.wait_ge(w_step, c * 12 + PRIMED)
                dve.tensor_scalar(magnitude[:], packed[:, m, :], 4 * nib, 7, ALU.logical_shift_right, ALU.bitwise_and).then_inc(dq_step, 1)
                dve.tensor_scalar(signed_scale[:, k % 2, :], packed[:, m, :], 28 - 4 * nib, -2 ** 31, ALU.logical_shift_left, ALU.bitwise_and).then_inc(dq_step, 1)
                dve.wait_ge(dq_step, base + 1)
                dve.tensor_scalar(lut_line[:], magnitude[:], 2.0, -8.0, ALU.mult, ALU.add).then_inc(dq_step, 1)
                dve.wait_ge(dq_step, base + 2)
                dve.tensor_tensor(signed_scale[:, k % 2, :], signed_scale[:, k % 2, :], scales[:, m, :].bitcast(I32), ALU.bitwise_xor).then_inc(dq_step, 1)
                dve.wait_ge(dq_step, base + 3)
                dve.scalar_tensor_tensor(lut_line[:], magnitude[:], -2.0, lut_line[:], ALU.add, ALU.max).then_inc(dq_step, 1)
                dve.wait_ge(dq_step, base + 5)
                dve.scalar_tensor_tensor(lut_v[:, k % 2, :], magnitude[:], 0.5, lut_line[:], ALU.mult, ALU.max).then_inc(dq_step, 1)

            def tile(tt, par):
                t = tt * 2 + par
                for c in range(KC):
                    dve.wait_ge(hs_hi, t * KC + c + 1)
                    bank = proj[use(f"hs{c}")[0]]
                    dve.tensor_tensor(hs[:, LO, c, :], bank[:], hs[:, HI, c, :].bitcast(F32), ALU.subtract).then_inc(proj_free[use(f"hs{c}")[0]], 1)

                def rope_turn(c):
                    evacuated(dve, t, ("k0", "k1", "q0", "q1", "q2", "q3")[c])
                    passed()
                    dve.stream_shuffle(rope_sin[:, c % 2, :], rope_in[:, c % 2, :], [(i + HD // 2) % HD for i in range(HD)]).then_inc(rope_turned, 1)

                def rope_add(c):
                    dve.wait_ge(rope_parts, t * 6 + c + 1)
                    dst = kT[:, c, :] if c < 2 else qT[:, c - 2, :]
                    dve.tensor_tensor(dst, rope_in[:, c % 2, :], rope_sin[:, c % 2, :], ALU.add).then_inc(rope_done, 1)

                for q in h_stored:
                    dve.wait_ge(q, t * (KC // 2) * 16 + PRIMED)
                passed()
                rope_turn(0)
                rope_turn(1)
                for c in range(2, 6):
                    rope_add(c - 2)
                    rope_turn(c)
                rope_add(4)
                rope_add(5)

                steps = 2 * TOPK // 8 + 1
                s0 = t * steps
                dve.wait_ge(z_ld, (t + 1) * 16)
                dve.tensor_scalar(rank[:], z_rows[:], SIGMOID_ONE, SIGMOID_ZERO, ALU.min, ALU.max).then_inc(topk_step, 1)
                for r in range(TOPK // 8):
                    dve.wait_ge(topk_step, s0 + 2 * r + 1)
                    passed()
                    dve.max(top8[:], rank[:]).then_inc(topk_step, 1)
                    dve.wait_ge(topk_step, s0 + 2 * r + 2)
                    passed()
                    dve.match_replace(rank[:], top8[:], rank[:], PICKED).then_inc(topk_step, 1)
                dve.wait_ge(topk_step, s0 + steps)
                dve.tensor_scalar(key_bias[:], rank[:], PICKED / 2, MASKED, ALU.is_gt, ALU.mult).then_inc(bias_ready, 1)

                def value(q):
                    bank = full_wait(dve, t, f"v{q}")
                    for b in range(2):
                        rows = slice(b * C, (b + 1) * C)
                        for r in range(2):
                            ins = dve.tensor_tensor(v_diag[r * C:(r + 1) * C, q % 2, b, :, r * HD:(r + 1) * HD],
                                                    bank[rows, 0:256].rearrange("p (g d) -> p g d", d=HD),
                                                    bv[rows, :].rearrange("p (g d) -> p g d", d=HD), ALU.add)
                    ins.then_inc(proj_free[use(f"v{q}")[0]], 1)

                def softmax_shift(q):
                    sc = scores[:].rearrange("p a h c -> p (a h) c")
                    dve.wait_ge(score_step, (t * NP + q) * 8 + 8)
                    dve.tensor_reduce(row_max[:, q % 2, :], sc, AX_X, ALU.max).then_inc(scores_max, 1)
                    dve.wait_ge(scores_max, t * NP + q + 1)
                    dve.tensor_tensor(probs[:, q % 2], sc, row_max[:, q % 2, :].unsqueeze(2).to_broadcast([P, HEADS, C]),
                                      ALU.subtract).then_inc(scores_used, 1)

                def normalise(q):
                    dve.wait_ge(exp_done, t * NP + q + 1)
                    dve.tensor_reduce(row_sum[:, q % 2, :], probs[:, q % 2], AX_X, ALU.add).then_inc(sum_step, 1)
                    dve.wait_ge(sum_step, (t * NP + q) * 2 + 1)
                    dve.reciprocal(row_inv[:, q % 2, :], row_sum[:, q % 2, :]).then_inc(sum_step, 1)
                    dve.wait_ge(sum_step, (t * NP + q) * 2 + 2)
                    dve.wait_ge(pv_full, t * NP + q + 1)
                    dve.tensor_tensor(heads_out[:, q % 2], pv[:].rearrange("p g (r d) -> p (g r) d", r=2),
                                      row_inv[:, q % 2, :].unsqueeze(2).to_broadcast([P, HEADS, HD]), ALU.mult).then_inc(pv_used, 1)

                def turn_low(name, parts):
                    n = TURNS.index(name)
                    dve.wait_ge(turn_hi, t * 8 + n + 1)
                    dve.tensor_tensor(parts(LO), turn[:], parts(HI).bitcast(F32), ALU.subtract).then_inc(turn_used, 1)

                for slot in range(SLOTS):
                    if slot < NP:
                        value(slot)
                        softmax_shift(slot)
                    if 1 <= slot <= NP:
                        normalise(slot - 1)
                    if 2 <= slot <= NP + 1:
                        q = slot - 2
                        turn_low(f"o{q}", lambda u: attnT[:, u])
                        bank = full_wait(dve, t, f"o{q}")
                        if q == 0:
                            dve.wait_ge(residual_ready, t + 1)
                        dve.tensor_tensor(x_in[:, par, q, :], bank[:], x_in[:, par, q, :], ALU.add).then_inc(proj_free[use(f"o{q}")[0]], 1)
                    if slot >= 3:
                        q = slot - 3
                        turn_low(f"x{q}", lambda u: x1T[:, u, :, q * P:(q + 1) * P])
                    if slot < 6:
                        dequantise(t, slot)

                bank = full_wait(dve, t, "xa")
                dve.tensor_tensor(xa[:].rearrange("p (b c) -> p b c", c=C), bank[:].rearrange("p (b c) -> p b c", c=C),
                                  adapter_mask[:, bass.ds(t * NB, NB)].unsqueeze(2).to_broadcast([P, NB, C]), ALU.mult).then_inc(proj_free[use("xa")[0]], 1)
                dve.wait_ge(xa_hi, t + 1)
                dve.tensor_tensor(xa_parts[:, LO, :], xa[:], xa_parts[:, HI, :].bitcast(F32), ALU.subtract).then_inc(xa_lo, 1)
                for n in range(KC):
                    dve.wait_ge(h_hi, t * KC + n + 1)
                    bank = proj[use(f"h{n}")[0]]
                    dve.tensor_tensor(h_out[:, n % 2, LO, :], bank[:], h_out[:, n % 2, HI, :].bitcast(F32), ALU.subtract).then_inc(proj_free[use(f"h{n}")[0]], 1)

            with dve.Fori(0, NT // 2) as tt:
                tile(tt, 0)
                tile(tt, 1)

            def add_down(i, pair, par):
                dve.wait_ge(acc_ld[par], (pair + 1) * 16)
                for tc in range(NP):
                    dve.wait_ge(down_full, i * NP + tc + 1)
                    dve.tensor_tensor(acc[par][:, tc, :], down[tc][:], acc[par][:, tc, :], ALU.add).then_inc(acc_added, 1)

            def ffn_tile(pair, par, first=False, block_c=None):
                i = pair * 2 + par
                for j in range(NS):
                    b = j % 2
                    n = i * NS + j + 1
                    dve.wait_ge(sq_done, n)
                    dve.scalar_tensor_tensor(gate_in[:], gate_sq[:], 1.0 / GELU_CUBIC, gate[b][:], ALU.add, ALU.mult).then_inc(gin_done, 1)
                    if block_c is not None and j < 6:
                        dequantise(block_c, j)
                    if j == 2 and not first:
                        add_down(i - 1, pair - 1 if par == 0 else pair, 1 - par)
                    dve.wait_ge(tanh_done, n)
                    dve.scalar_tensor_tensor(gate_val[:], gate_tanh[:], 1.0, gate[b][:], ALU.add, ALU.mult).then_inc(gval_done, 1)
                    dve.wait_ge(gval_done, n)
                    dve.wait_ge(up_full[b], i * (NS // 2) + j // 2 + 1)
                    dve.scalar_tensor_tensor(inter[:], gate_val[:], 0.5, up[b][:], ALU.mult, ALU.mult).then_inc(inter_done, 1)
                    dve.wait_ge(inter_hi, n)
                    dve.tensor_tensor(inter_parts[:, b, LO, :], inter[:], inter_parts[:, b, HI, :].bitcast(F32), ALU.subtract).then_inc(inter_ready, 1)

            NPAIR = NT // 2
            ffn_tile(0, 0, first=True, block_c=NT)
            ffn_tile(0, 1, block_c=NT + 1)
            with dve.Fori(1, NPAIR) as p:
                ffn_tile(p, 0, block_c=p * 2 + NT)
                ffn_tile(p, 1, block_c=p * 2 + NT + 1)
            with dve.Fori(NPAIR, NG * NPAIR) as p:
                ffn_tile(p, 0)
                ffn_tile(p, 1)
            add_down(NG * NT - 1, NG * NPAIR - 1, 1)


def rope_tables(C):
    inv_freq = (1.0 / ROPE_THETA ** (np.arange(0, HD, 2, dtype=np.float32) / HD)).astype(np.float32)
    freqs = np.arange(C, dtype=np.float32)[:, None] * inv_freq[None, :]
    emb = np.concatenate([freqs, freqs], axis=-1)
    cos, sin = np.cos(emb).astype(np.float32), np.sin(emb).astype(np.float32)
    sin = np.concatenate([-sin[:, :HD // 2], sin[:, HD // 2:]], axis=-1)
    return np.ascontiguousarray(np.tile(cos.T, (4, 1))), np.ascontiguousarray(np.tile(sin.T, (4, 1)))


def kernel(**inputs):
    import numpy as np
    import concourse.bacc as bacc
    from concourse import mybir
    from concourse.bass_utils import run_bass_kernel_spmd

    def get(name):
        return np.asarray(inputs[name])

    x = get("x")
    B, C, D = x.shape
    MLP = get("L0_ffn_gate_W_packed").shape[0]
    NCP = MLP // 256
    NB = TILE // C

    def head_order(w):
        lead = w.shape[:-1]
        w = w.reshape(*lead, 2, 4, 2, HD)
        return np.moveaxis(w, -2, -3).reshape(*lead, HEADS * HD)

    def nibble_order(w):
        lead = w.shape[:-1]
        return np.swapaxes(w.reshape(*lead, 2, P, 2), -1, -2).reshape(*lead, D)

    def channel_order(w):
        r = w.shape[0]
        return w.reshape(r, NCP, P, 2).transpose(1, 0, 3, 2).reshape(NCP, r, 256)

    def gate_pack(w):
        return channel_order(w.T).reshape(NCP, 2, P, 256).transpose(0, 2, 1, 3).reshape(NCP, P, 512)

    cos, sin = rope_tables(C)
    pair_rows = np.zeros((NB, NB // 2, P), np.float32)
    for b in range(NB):
        pair_rows[b, b // 2, (b % 2) * C:(b % 2 + 1) * C] = 1.0
    columns = np.stack([np.arange(P) % C, np.arange(P) // RANK], axis=1).astype(np.float32)
    arrays = {
        "x": x,
        "cond_index": get("itok_B_1_198").reshape(B // 2, 2).T,
        "adapter_index": get("itok_B_0_6")[None, :],
        "cond_weights": get("L0_cond_weights"),
        "wq": head_order(get("L0_attn_Wq")),
        "bq": head_order(get("L0_attn_bq")).reshape(4, P).T,
        "wk": get("L0_attn_Wk"),
        "bk": get("L0_attn_bk").reshape(2, P).T,
        "wv": get("L0_attn_Wv"),
        "bv": get("L0_attn_bv")[None, :],
        "wo": get("L0_attn_Wo"),
        "bo": get("L0_attn_bo")[None, :],
        "wr": get("L0_attn_Wr"),
        "br": get("L0_attn_br")[:, None],
        "w2": nibble_order(get("L0_cond2_W").T),
        "wa": get("L0_cond2_A").reshape(ADAPTERS * RANK, D).T,
        "wb": nibble_order(get("L0_cond2_Bm").transpose(0, 2, 1).reshape(ADAPTERS * RANK, D)),
        "adapter_scales": np.repeat(get("L0_cond2_scalings"), RANK)[:, None],
        "gate_packed": gate_pack(get("L0_ffn_gate_W_packed")),
        "gate_scales": channel_order(get("L0_ffn_gate_scales").T),
        "up_packed": gate_pack(get("L0_ffn_up_W_packed")),
        "up_scales": channel_order(get("L0_ffn_up_scales").T),
        "down_packed": get("L0_ffn_down_W_packed").T.reshape(NCP, P, D),
        "down_scales": get("L0_ffn_down_scales").T.reshape(NCP, 8, D),
        "cos": cos, "sin": sin,
        "identity": np.eye(P, dtype=np.float32),
        "pair_rows": pair_rows,
        "columns": columns,
    }
    nc = bacc.Bacc("TRN2", target_bir_lowering=False, num_devices=1)
    given, aps = {}, {}
    for name, v in arrays.items():
        v = np.ascontiguousarray(v)
        given["in_" + name] = v
        aps[name] = nc.dram_tensor("in_" + name, v.shape, mybir.dt.from_np(v.dtype), kind="ExternalInput").ap()
    out = nc.dram_tensor("out_0", (B, C, D), mybir.dt.float32, kind="ExternalOutput").ap()
    build(nc, aps, out)
    r = run_bass_kernel_spmd(nc, [given], core_ids=[0])
    return r.results[0]["out_0"]
```

```python
from contextlib import ExitStack

import numpy as np

import concourse.bass as bass
from concourse import mybir

F32 = mybir.dt.float32
F32R = mybir.dt.float32r
I32 = mybir.dt.int32
U32 = mybir.dt.uint32
BF16 = mybir.dt.bfloat16
ALU = mybir.AluOpType
ACT = mybir.ActivationFunctionType
AX_X = mybir.AxisListType.X

P = 128
HEADS, KV_HEADS, HD = 16, 8, 32
ROPE_THETA = 1000000.0
RANK, ADAPTERS = 16, 8
TOK = 256
TILE = 512
SIGMOID_ONE = 24 * float(np.log(2.0))
SIGMOID_ZERO = -88.72
PICKED = -1.0e30
MASKED = -1.0e30
GELU_CUBIC = 0.044715
GELU_SCALE = 0.7978845608028654
HI, LO = 0, 1


def split_product(passes):
    return [(HI, HI), (HI, LO), (LO, HI)]


THREE = split_product(3)


def build(nc, a, out):
    B, C, D = a["x"].shape
    NCP = a["gate_packed"].shape[0]
    KC = D // P
    NB = TOK // C
    NP = NB // 2
    NT = B // NB
    NF = B * C // TILE
    NQ = TILE // P
    GB = 4
    NG = NCP // GB
    NS = 2 * GB
    TOPK = C // 2
    assert D == TILE and C == 64 and NCP >= 2 * GB and NT % 2 == 0 and NF >= 4 and NCP == 2 * NF and NT == 2 * NF
    ATT_SCALE = HD ** -0.5

    h_scr = nc.dram_tensor("h_scratch", (NF, P, KC, 2, TILE), F32, kind="Internal").ap()
    w_scr = nc.dram_tensor("w_scratch", (NCP, P, 3, 2, 2, 512), F32, kind="Internal").ap()
    z_scr = nc.dram_tensor("z_scratch", (NT, NB, HEADS, C), F32, kind="Internal").ap()
    m_scr = nc.dram_tensor("m_scratch", (NT, NB, HEADS, C), BF16, kind="Internal").ap()

    x_v = a["x"].rearrange("(t q b) c d -> t (b c) q d", q=NP, b=2)
    x1_v = out.rearrange("(t q b) c d -> t (b c) q d", q=NP, b=2)
    out_tiles = out.rearrange("(t q b) c d -> t (b c) q d", q=NQ, b=2)
    cond_rows = a["cond_weights"].rearrange("s c d -> (s c) d")

    with ExitStack() as ctx:
        def sem(name):
            return ctx.enter_context(nc.semaphore(name))

        def sb_in(stack):
            return lambda name, shape, dt: stack.enter_context(nc.sbuf_tensor(name, shape, dt))

        def ps_in(stack):
            return lambda name, shape, dt: stack.enter_context(nc.psum_tensor(name, shape, dt))

        sb = sb_in(ctx)
        packed = sb("packed", [P, 3, 512], I32)
        scales = sb("scales", [P, 3, 512], F32)
        magnitude = sb("magnitude", [P, 512], I32)
        signed_scale = sb("signed_scale", [P, 2, 512], I32)
        lut_line = sb("lut_line", [P, 512], F32)
        lut_v = sb("lut_v", [P, 2, 512], F32)
        w_parts = sb("w_parts", [P, 2, 2, 512], F32R)

        with ExitStack() as token_stage:
            sb = sb_in(token_stage)
            ps = ps_in(token_stage)
            wq = sb("wq", [P, 2, KC, 512], F32R)
            wk = sb("wk", [P, 2, KC, 256], F32R)
            wv = sb("wv", [P, 2, KC, 256], F32R)
            wo = sb("wo", [P, 2, KC, 512], F32R)
            w2 = sb("w2", [P, 2, KC, 512], F32R)
            wr = sb("wr", [P, 2, KC, HEADS], F32R)
            wa = sb("wa", [P, 2, KC, P], F32R)
            wb = sb("wb", [P, 2, 512], F32R)
            bq = sb("bq", [P, 4], F32)
            bk = sb("bk", [P, 2], F32)
            bv = sb("bv", [P, 256], F32)
            bo = sb("bo", [P, 512], F32)
            br = sb("br", [HEADS, 1], F32)
            cos = sb("cos", [P, C], F32)
            sin = sb("sin", [P, C], F32)
            identity = sb("identity", [P, P], F32)
            batch_rows_f = sb("batch_rows_f", [2 * NB, NB, P], F32)
            batch_rows = sb("batch_rows", [2 * NB, NB, P], BF16)
            columns = sb("columns", [P, 2], F32)
            adapter_of = sb("adapter_of", [P, B], I32)
            adapter_scale = sb("adapter_scale", [P, 1], F32)
            adapter_mask = sb("adapter_mask", [P, B], F32)
            cond_of = sb("cond_of", [P, B // 2], I32)
            cond_row = sb("cond_row", [P, B // 2], U32)
            mix = sb("mix", [P, B // 2, C], F32)
            mix_tile = sb("mix_tile", [P, 2, NP, 2, C], F32)
            x_in = sb("x_in", [P, 2, NP, D], F32)
            x1 = sb("x1", [P, NP, D], F32)
            hs = sb("hs", [P, 2, KC, TOK], F32R)
            z_sb = sb("z_sb", [HEADS, TOK], F32)
            z_rows = sb("z_rows", [NB * HEADS, C], F32)
            rank = sb("rank", [NB * HEADS, C], F32)
            top8 = sb("top8", [NB * HEADS, 8], F32)
            key_bias = sb("key_bias", [NB * HEADS, C], BF16)
            bias_rows = sb("bias_rows", [2 * NB, KV_HEADS * C], BF16)
            rope_in = sb("rope_in", [P, 2, TOK], F32)
            rope_sin = sb("rope_sin", [P, 2, TOK], F32)
            qT = sb("qT", [P, 2, NB, 2, C], F32)
            kT = sb("kT", [P, 2, TOK], F32)
            v_sb = sb("v_sb", [P, 2, NP, KV_HEADS, HD], F32)
            with ExitStack() as staging:
                w_stage = sb_in(staging)("w_stage", [P, 2, KC, 512], F32)
            probs = sb("probs", [P, NP, KV_HEADS, 2, C], F32)
            probsT = sb("probsT", [P, KV_HEADS, P], F32)
            attnT = sb("attnT", [P, NP, 2, KC, P], F32R)
            row_max = sb("row_max", [P, NP, 2, KV_HEADS], F32)
            row_sum = sb("row_sum", [P, NP, 2, KV_HEADS], F32)
            row_inv = sb("row_inv", [P, NP, 2, KV_HEADS], F32)
            x1T = sb("x1T", [P, 2, KC, TOK], F32R)
            xa = sb("xa", [P, TOK], F32)
            xa_parts = sb("xa_parts", [P, 2, TOK], F32R)
            h_out = sb("h_out", [P, 2, 2, TOK], F32R)
            proj = [ps(f"proj{i}", [P, 512], F32) for i in range(2)]
            scores = ps("scores", [P, 2, KV_HEADS, C], F32)
            pT = ps("pT", [P, KV_HEADS, P], F32)
            pv = ps("pv", [P, 2, 2, 2, C], F32)
            turn = ps("turn", [P, KC, P], F32)

        with ExitStack() as ffn_stage:
            sb = sb_in(ffn_stage)
            ps = ps_in(ffn_stage)
            w_slot = [sb(f"w_slot{k}", [P, 3, 2, 2, 512], F32R) for k in range(GB)]
            h_in = [sb(f"h_in{k}", [P, KC, 2, TILE], F32R) for k in range(2)]
            acc = [sb(f"acc{k}", [P, NQ, D], F32) for k in range(2)]
            gate_sq = sb("gate_sq", [P, TILE], F32)
            gate_in = sb("gate_in", [P, TILE], F32)
            gate_tanh = sb("gate_tanh", [P, TILE], F32)
            gate_val = sb("gate_val", [P, TILE], F32)
            inter = sb("inter", [P, TILE], F32)
            inter_parts = sb("inter_parts", [P, 2, 2, TILE], F32R)
            down = [ps(f"down{i}", [P, D], F32) for i in range(NQ)]
            gate = [ps(f"gate{i}", [P, TILE], F32) for i in range(2)]
            up = [ps(f"up{i}", [P, TILE], F32) for i in range(2)]

        index_ld = sem("index_ld")
        const_ld = sem("const_ld")
        const_made = sem("const_made")
        cond_row_ready = sem("cond_row_ready")
        gather_first, gather_rest = sem("gather_first"), sem("gather_rest")
        raw_ld = [sem("raw_ld0"), sem("raw_ld1")]
        raw_hi, raw_lo = sem("raw_hi"), sem("raw_lo")
        mix_cleared, mix_ready = sem("mix_cleared"), sem("mix_ready")
        score_step, pv_step = sem("score_step"), sem("pv_step")
        x_ld = [sem("x_ld0"), sem("x_ld1")]
        proj_full = [sem("proj_full0"), sem("proj_full1")]
        proj_free = [sem("proj_free0"), sem("proj_free1")]
        hs_hi = sem("hs_hi")
        z_stored, z_ld = sem("z_stored"), sem("z_ld")
        topk_step, bias_ready, bias_stored, bias_ld = sem("topk_step"), sem("bias_ready"), sem("bias_stored"), sem("bias_ld")
        rope_step, rope_done = sem("rope_step"), sem("rope_done")
        scores_max, scores_used = sem("scores_max"), sem("scores_used")
        exp_done, sum_step, probs_ready = sem("exp_done"), sem("sum_step"), sem("probs_ready")
        pT_full, pT_used = sem("pT_full"), sem("pT_used")
        pv_full, pv_hi, pv_used = sem("pv_full"), sem("pv_hi"), sem("pv_used")
        turn_full, turn_hi, turn_used = sem("turn_full"), sem("turn_hi"), sem("turn_used")
        residual_ready, x1_stored = sem("residual_ready"), sem("x1_stored")
        xa_hi, xa_lo = sem("xa_hi"), sem("xa_lo")
        h_hi = sem("h_hi")
        h_stored = [sem("h_stored0"), sem("h_stored1")]
        packed_ld = [sem(f"packed_ld{m}") for m in range(3)]
        dq_step, w_used, w_step = sem("dq_step"), sem("w_used"), sem("w_step")
        w_stored = [sem("w_stored0"), sem("w_stored1")]
        pool_passed = sem("pool_passed")
        dve_passed = sem("dve_passed")
        pe_passed = sem("pe_passed")
        sp_passed = sem("sp_passed")
        slot_ld = [sem(f"slot_ld{k}") for k in range(GB)]
        h_ld = [sem("h_ld0"), sem("h_ld1")]
        acc_ld = [sem("acc_ld0"), sem("acc_ld1")]
        acc_stored = [sem("acc_stored0"), sem("acc_stored1")]
        gate_full = [sem("gate_full0"), sem("gate_full1")]
        up_full = [sem("up_full0"), sem("up_full1")]
        down_done, down_full, acc_added = sem("down_done"), sem("down_full"), sem("acc_added")
        sq_done, gin_done, tanh_done, gval_done = sem("sq_done"), sem("gin_done"), sem("tanh_done"), sem("gval_done")
        inter_done, inter_hi, inter_ready = sem("inter_done"), sem("inter_hi"), sem("inter_ready")

        TAIL = ["xa", "h0", "h1", "h2", "h3"]
        HEAD = ["hs0", "hs1", "hs2", "hs3", "z", "k0", "k1", "q0", "q1", "q2", "q3", "v0", "v1"]
        USES = ["hs0", "hs1", "hs2", "hs3", "xa", "z", "h0", "h1", "h2", "h3", "k0", "k1", "q0", "q1", "o0",
                "q2", "q3", "o1", "v0", "v1"]
        BANK = {name: n % 2 for n, name in enumerate(USES)}
        ROPE = ("k0", "k1", "q0", "q1", "q2", "q3")

        PRIMED = 1
        FIRST, AHEAD, BEHIND = 0, "ahead", "behind"

        def uses_before(it, name):
            bank = BANK[name]

            def count(names):
                return sum(BANK[x] == bank for x in names)

            if isinstance(it, str) and it == AHEAD:
                return count(HEAD[:HEAD.index(name)])
            before = USES[:USES.index(name)]
            if isinstance(it, int) and it == 0:
                return count(HEAD) + count([x for x in before if x not in TAIL])
            start = count(HEAD) - count(TAIL)
            if isinstance(it, str) and it == BEHIND:
                return start + (NT - 1) * count(USES) + count(TAIL) + count(["o0", "o1"]) + count(TAIL[:TAIL.index(name)])
            if isinstance(it, int) and it == NT - 1:
                return start + it * count(USES) + count([x for x in before if x not in HEAD])
            return start + it * count(USES) + count(before)

        def full_wait(eng, it, name):
            eng.wait_ge(proj_full[BANK[name]], uses_before(it, name) + 1)
            return proj[BANK[name]]

        def evacuated(eng, it, name):
            eng.wait_ge(proj_free[BANK[name]], uses_before(it, name) + 1 + PRIMED)

        RAW = [("wr", wr, HEADS), ("wk", wk, 256), ("wq", wq, 512), ("wv", wv, 256),
               ("wo", wo, 512), ("w2", w2, 512), ("wa", wa, P), ("wb", wb, None)]
        SPLIT = {name: j + 1 for j, (name, _, _) in enumerate(RAW)}
        N_CONST = 11

        stages = [w_stage[:, n] for n in range(2)]

        def raw_views(j):
            _, parts, cols = RAW[j]
            stage = stages[j % 2]
            if cols is None:
                return stage[:, 0, :], parts[:, HI, :], parts[:, LO, :]
            return stage[:, :, 0:cols], parts[:, HI], parts[:, LO]

        block = ctx.enter_context(nc.Block())

        @block.sync
        def _(sp):
            for q in (*h_stored, x1_stored):
                sp.sem_inc(q, PRIMED)
            def passed():
                sp.sem_inc(sp_passed, 1)

            sp.dma_start(cond_of[0:C, :], a["cond_index"][0:1, :].to_broadcast([C, B // 2])).then_inc(index_ld, 16)
            sp.dma_start(cond_of[C:P, :], a["cond_index"][1:2, :].to_broadcast([C, B // 2])).then_inc(index_ld, 16)
            sp.dma_start(columns[:], a["columns"]).then_inc(index_ld, 16)
            sp.dma_start(x_in[:, 0], x_v[0]).then_inc(x_ld[0], 16)

            def load_raw(j):
                name, _, cols = RAW[j]
                if j >= 2:
                    sp.wait_ge(raw_lo, j - 1)
                sp.dma_start(raw_views(j)[0], a[name] if cols is None else a[name].rearrange("(k p) n -> p k n", p=P)).then_inc(raw_ld[j % 2], 16)

            load_raw(0)
            load_raw(1)
            for dst, src in ((bq, a["bq"]), (bk, a["bk"]), (cos, a["cos"]), (sin, a["sin"]),
                             (identity, a["identity"]), (batch_rows_f, a["batch_rows"]), (br, a["br"])):
                sp.dma_start(dst[:], src).then_inc(const_ld, 16)
            sp.dma_start(bv[:], a["bv"].to_broadcast([P, 256])).then_inc(const_ld, 16)
            sp.dma_start(bo[:], a["bo"].to_broadcast([P, 512])).then_inc(const_ld, 16)
            sp.dma_start(adapter_of[:], a["adapter_index"].to_broadcast([P, B])).then_inc(const_ld, 16)
            sp.dma_start(adapter_scale[:], a["adapter_scales"]).then_inc(const_ld, 16)
            sp.dma_start(x_in[:, 1], x_v[1]).then_inc(x_ld[1], 16)
            load_raw(2)
            load_raw(3)

            def route(it, t):
                evacuated(sp, it, "z")
                passed()
                sp.dma_start(z_scr[t].rearrange("b h c -> h b c"), z_sb[:].rearrange("h (b c) -> h b c", c=C)).then_inc(z_stored, 16)
                sp.wait_ge(z_stored, (t + 1) * 16)
                passed()
                sp.dma_start(z_rows[:], z_scr[t].rearrange("b h c -> (b h) c")).then_inc(z_ld, 16)

            def bias(t):
                sp.wait_ge(bias_ready, t + 1)
                passed()
                sp.dma_start(m_scr[t].rearrange("b h c -> (b h) c"), key_bias[:]).then_inc(bias_stored, 16)
                sp.wait_ge(bias_stored, (t + 1) * 16)
                passed()
                sp.dma_start(bias_rows[:], m_scr[t].rearrange("b (r g) c -> (b r) (g c)", r=2)).then_inc(bias_ld, 16)

            def tail(it, f, half):
                for n in range(KC):
                    evacuated(sp, it, f"h{n}")
                    passed()
                    sp.dma_start(h_scr[f, :, n, :, half * TOK:(half + 1) * TOK], h_out[:, n % 2].bitcast(F32)).then_inc(h_stored[n % 2], 16)

            def iteration(it, f, par, more_x=True):
                t = it
                if more_x:
                    sp.wait_ge(residual_ready, t + 1)
                    passed()
                    sp.dma_start(x_in[:, par], x_v[t + 2]).then_inc(x_ld[par], 16)
                last = isinstance(it, int) and it == NT - 1
                if not last:
                    route(it, t + 1)
                if f is not None:
                    tail(it, f, 1 - par)
                if not last:
                    bias(t + 1)
                evacuated(sp, it, "o0")
                passed()
                evacuated(sp, it, "o1")
                passed()
                sp.dma_start(x1_v[t], x1[:]).then_inc(x1_stored, 16)

            route(AHEAD, 0)
            load_raw(4)
            load_raw(5)
            bias(0)
            load_raw(6)
            load_raw(7)
            iteration(0, None, 0)
            with sp.Fori(0, NT // 2 - 2) as n:
                iteration(n * 2 + 1, n, 1)
                iteration(n * 2 + 2, n, 0)
            iteration(NT - 3, NF - 2, 1)
            iteration(NT - 2, NF - 2, 0, more_x=False)

            evacuated(sp, NT - 2, "v0")
            evacuated(sp, NT - 2, "v1")
            for q in w_stored:
                sp.wait_ge(q, 48)
            sp.dma_start(w_slot[0][:].bitcast(F32), w_scr[0]).then_inc(slot_ld[0], 16)
            iteration(NT - 1, NF - 1, 1, more_x=False)
            tail(BEHIND, NF - 1, 1)

            for q in h_stored:
                sp.wait_ge(q, NT * (KC // 2) * 16 + PRIMED)
            sp.wait_ge(x1_stored, NT * 16 + PRIMED)

            def load_slot(g, k):
                sp.dma_start(w_slot[k][:].bitcast(F32), w_scr[g * GB + k]).then_inc(slot_ld[k], 16)

            def load_tile(s, par):
                sp.dma_start(h_in[par][:].bitcast(F32), h_scr[s]).then_inc(h_ld[par], 16)

            def load_acc(s, par):
                sp.dma_start(acc[par][:], out_tiles[s]).then_inc(acc_ld[par], 16)

            load_tile(0, 0)
            for q in w_stored:
                sp.wait_ge(q, GB * 48)
            for k in range(1, GB):
                load_slot(0, k)
            load_acc(0, 0)
            load_tile(1, 1)
            load_acc(1, 1)

            def store(i, s, par):
                sp.wait_ge(acc_added, (i + 1) * NQ)
                passed()
                sp.dma_start(out_tiles[s], acc[par][:]).then_inc(acc_stored[par], 16)

            def step(pair, i, s_before, s_next):
                sp.wait_ge(down_done, i * (NS - 1) - 1)
                passed()
                load_tile(s_next, 1)
                store(i - 1, s_before, 1)
                sp.wait_ge(acc_stored[1], pair * 16)
                passed()
                load_acc(s_next, 1)

            NPAIR = NF // 2

            def pair_body(g, p, first=False, last_of_group=False, very_last=False):
                pair = g * NPAIR + p
                i0 = pair * 2
                s0 = p * 2
                wrap_before = (NF - 1) if (isinstance(p, int) and p == 0) else s0 - 1
                if not first:
                    step(pair, i0, wrap_before, s0 + 1)
                i1 = i0 + 1
                s_next = 0 if last_of_group else s0 + 2
                if very_last:
                    store(i1 - 1, s0, 0)
                    return
                sp.wait_ge(down_done, i1 * (NS - 1) - 1)
                passed()
                load_tile(s_next, 0)
                if last_of_group:
                    weights_stored((g + 2) * GB)
                    for k in range(GB):
                        if k == GB - 1:
                            store(i1 - 1, s0, 0)
                        if k < GB - 1:
                            sp.wait_ge(down_done, i1 * (NS - 1) + 2 * k + 2)
                        else:
                            sp.wait_ge(down_full, (i1 + 1) * NQ)
                        passed()
                        load_slot(g + 1, k)
                else:
                    store(i1 - 1, s0, 0)
                sp.wait_ge(acc_stored[0], (pair + 1) * 16)
                passed()
                load_acc(s_next, 0)

            def weights_stored(blocks):
                for q in w_stored:
                    sp.wait_ge(q, blocks * 48)
                    passed()

            def group(g, last_group):
                if isinstance(g, int) and g == 0:
                    pair_body(0, 0, first=True)
                else:
                    pair_body(g, 0)
                if NPAIR > 2:
                    with sp.Fori(1, NPAIR - 1) as p:
                        pair_body(g, p)
                pair_body(g, NPAIR - 1, last_of_group=True, very_last=last_group)

            group(0, NG == 1)
            if NG > 2:
                with sp.Fori(1, NG - 1) as g:
                    group(g, False)
            group(NG - 1, True)
            i_last = NG * NF - 1
            sp.wait_ge(acc_added, (i_last + 1) * NQ)
            sp.dma_start(out_tiles[NF - 1], acc[1][:]).then_inc(acc_stored[1], 16)
            sp.wait_ge(acc_stored[0], NG * NPAIR * 16)
            sp.wait_ge(acc_stored[1], NG * NPAIR * 16)

        @block.gpsimd
        def _(pool):
            pool.sem_inc(w_step, PRIMED)

            def passed():
                pool.sem_inc(pool_passed, 1)

            def load_packed(c, m):
                name = ("gate", "up", "down")[m]
                pool.dma_start(packed[:, m, :], a[name + "_packed"][c]).then_inc(packed_ld[m], 16)
                if m < 2:
                    for k in range(2):
                        pool.dma_start(scales[:, m, k * 256:(k + 1) * 256],
                                       a[name + "_scales"][c, 8 * k:8 * k + 8, :].unsqueeze(1).to_broadcast([8, 16, 256])).then_inc(packed_ld[m], 16)
                else:
                    pool.dma_start(scales[:, m, :], a[name + "_scales"][c].unsqueeze(1).to_broadcast([8, 16, 512])).then_inc(packed_ld[m], 16)

            pool.wait_ge(cond_row_ready, 1)
            for q in range(B // 2):
                pool.indirect_dma_start(mix[:, q, :], None, cond_rows, bass.IndirectOffsetOnAxis(ap=cond_row[:, q:q + 1], axis=0)) \
                    .then_inc(gather_first if q < NP else gather_rest, 16)
            for m in range(3):
                load_packed(0, m)

            def weight_block(c, k, last):
                m, nib = k // 2, k % 2
                par = k % 2
                pool.wait_ge(dq_step, c * 36 + 6 * k + 6)
                pool.tensor_tensor(lut_v[:, par, :], lut_v[:, par, :], signed_scale[:, par, :].bitcast(F32), ALU.mult).then_inc(w_used, 1)
                if nib == 1 and not last:
                    load_packed(c + 1, m)
                if k >= 2:
                    pool.wait_ge(w_stored[par], (c * 3 + m) * 16)
                    passed()
                pool.wait_ge(w_used, c * 6 + k + 1)
                passed()
                pool.tensor_copy(w_parts[:, par, HI, :], lut_v[:, par, :]).then_inc(w_step, 1)
                pool.wait_ge(w_step, c * 12 + 2 * k + 1 + PRIMED)
                pool.tensor_tensor(w_parts[:, par, LO, :], lut_v[:, par, :], w_parts[:, par, HI, :].bitcast(F32), ALU.subtract).then_inc(w_step, 1)
                pool.wait_ge(w_step, c * 12 + 2 * k + 2 + PRIMED)
                passed()
                pool.dma_start(w_scr[c, :, m, nib], w_parts[:, par].bitcast(F32)).then_inc(w_stored[par], 16)
                if k == 5:
                    for q in w_stored:
                        pool.wait_ge(q, (c + 1) * 48)
                        passed()

            def iteration(t, par, c, k0):
                pool.wait_ge(x1_stored, t * 16 + PRIMED)
                passed()
                pool.wait_ge(turn_used, t * NP + PRIMED)
                passed()
                for q in range(NP):
                    ins = pool.tensor_tensor(x1[:, q, :], x_in[:, par, q, :], bo[:], ALU.add)
                ins.then_inc(residual_ready, 1)
                for n in range(3):
                    weight_block(c, k0 + n, False)

            pool.wait_ge(const_ld, N_CONST * 16)
            pool.wait_ge(x_ld[0], 16)
            iteration(0, 0, 0, 0)
            with pool.Fori(0, NT // 2 - 1) as n:
                iteration(n * 2 + 1, 1, n, 3)
                iteration(n * 2 + 2, 0, n + 1, 0)
            iteration(NT - 1, 1, NT // 2 - 1, 3)
            with pool.Fori(NF, NCP - 1) as c:
                for k in range(6):
                    weight_block(c, k, False)
            for k in range(6):
                weight_block(NCP - 1, k, True)
            for q in w_stored:
                pool.wait_ge(q, NCP * 48)

        @block.tensor
        def _(pe):
            def passed():
                pe.sem_inc(pe_passed, 1)

            def ready(it, name):
                pe.wait_ge(proj_free[BANK[name]], uses_before(it, name) + PRIMED)
                return proj[BANK[name]], proj_full[BANK[name]]

            def products(out_ap, pairs, start=True, stop=True):
                for n, (lhsT, rhs) in enumerate(pairs):
                    ins = pe.matmul(out_ap, lhsT, rhs, start=(start and n == 0), stop=(stop and n == len(pairs) - 1))
                return ins

            def mixing(it, t, tt, par, chunks):
                pe.wait_ge(x_ld[par], (tt + 1) * 16)
                pe.wait_ge(mix_ready, t * 2 + 2)
                for c in chunks:
                    bank, done = ready(it, f"hs{c}")
                    for q in range(NP):
                        ins = pe.matmul(bank[:, q * P:(q + 1) * P], x_in[:, par, q, c * P:(c + 1) * P],
                                        mix_tile[:, par, q].rearrange("p b c -> p (b c)"), start=True, stop=True)
                    ins.then_inc(done, 1)

            def routing(it):
                bank, done = ready(it, "z")
                evacuated(pe, it, "hs2")
                evacuated(pe, it, "hs3")
                products(bank[0:HEADS, 0:TOK], [(wr[:, i, c, :], hs[:, j, c, :]) for c in range(KC) for i, j in THREE]).then_inc(done, 1)

            def project(it, name, w):
                bank, done = ready(it, name)
                n = int(name[1])
                products(bank[:, 0:TOK], [(w[:, i, c, n * P:(n + 1) * P], hs[:, j, c, :]) for c in range(KC) for i, j in THREE]).then_inc(done, 1)

            def value(it, q):
                bank, done = ready(it, f"v{q}")
                products(bank[:, 0:256], [(hs[:, i, c, q * P:(q + 1) * P], wv[:, j, c, :]) for c in range(KC) for i, j in THREE]).then_inc(done, 1)

            def score(t, q):
                pe.wait_ge(scores_used, t * NP + q + PRIMED)
                for b in range(2):
                    pe.matmul(scores[:, b].rearrange("p g c -> p (g c)"), batch_rows[:, 2 * q + b, :], bias_rows[:],
                              start=True, stop=False, skip_group_check=True)
                for i in range(4):
                    for b in range(2):
                        if i > 0:
                            pe.wait_ge(score_step, (t * NP + q) * 8 + 2 * (i - 1) + b + 1)
                        cols = slice(q * P + b * C, q * P + (b + 1) * C)
                        for gc in range(2):
                            ins = pe.matmul(scores[:, b, 4 * gc + i, :], qT[32 * i:32 * i + 32, gc, 2 * q + b].rearrange("p r c -> p (r c)"),
                                            kT[32 * i:32 * i + 32, gc, cols], start=False, stop=True,
                                            skip_group_check=True, tile_position=(32 * i, 0))
                        ins.then_inc(score_step, 1)

            def turn_probs(t, q):
                pe.wait_ge(probs_ready, t * NP + q + 1)
                pe.wait_ge(pT_used, t * NP + q + PRIMED)
                for g in range(KV_HEADS):
                    ins = pe.transpose(pT[:, g, :], probs[:, q, g].rearrange("p b c -> p (b c)"), identity[:])
                ins.then_inc(pT_full, 1)

            def attend(t, par, q):
                pe.wait_ge(pT_used, t * NP + q + 1 + PRIMED)
                pe.wait_ge(pv_used, t * NP + q + PRIMED)
                if q == 0:
                    evacuated(pe, t - 1 if not (isinstance(t, int) and t == 0) else AHEAD, "v0")
                    evacuated(pe, t - 1 if not (isinstance(t, int) and t == 0) else AHEAD, "v1")
                passed()
                for b in range(2):
                    if b == 1:
                        pe.wait_ge(pv_step, t * NP + q + 1)
                        passed()
                    rows = slice(b * C, (b + 1) * C)
                    for g in range(KV_HEADS):
                        gc, i = g // 4, g % 4
                        ins = pe.matmul(pv[32 * i:32 * i + 32, gc, :, b, :], v_sb[rows, par, q, g, :], probsT[rows, g, :],
                                        start=True, stop=True, tile_position=(b * C, 32 * i))
                    ins.then_inc(pv_step if b == 0 else pv_full, 1)

            def turn_rows(it, t, q):
                evacuated(pe, it, f"o{q}")
                pe.wait_ge(turn_used, t * NP + q + PRIMED)
                for c in range(KC):
                    ins = pe.transpose(turn[:, c, :], x1[:, q, c * P:(c + 1) * P], identity[:])
                ins.then_inc(turn_full, 1)

            def out_proj(it, t, q):
                bank, done = ready(it, f"o{q}")
                pe.wait_ge(pv_used, t * NP + q + 1 + PRIMED)
                products(bank[:], [(attnT[:, q, i, c, :], wo[:, j, c, :]) for c in range(KC) for i, j in THREE]).then_inc(done, 1)

            def adapter_ranks(it, t):
                bank, done = ready(it, "xa")
                pe.wait_ge(turn_used, (t + 1) * NP + PRIMED)
                products(bank[:, 0:TOK], [(wa[:, i, c, :], x1T[:, j, c, :]) for c in range(KC) for i, j in THREE]).then_inc(done, 1)

            def hidden_main(it, n):
                bank, done = ready(it, f"h{n}")
                products(bank[:, 0:TOK], [(w2[:, i, c, n * P:(n + 1) * P], x1T[:, j, c, :]) for c in range(KC) for i, j in THREE], stop=False)

            def hidden_adapter(n):
                products(proj[BANK[f"h{n}"]][:, 0:TOK], [(wb[:, i, n * P:(n + 1) * P], xa_parts[:, j, :]) for i, j in THREE],
                         start=False).then_inc(proj_full[BANK[f"h{n}"]], 1)

            def hidden_first(it, t):
                hidden_main(it, 0)
                hidden_main(it, 1)
                pe.wait_ge(xa_lo, t + 1)
                hidden_adapter(0)
                hidden_adapter(1)

            def hidden_rest(it):
                for n in (2, 3):
                    hidden_main(it, n)
                    hidden_adapter(n)

            def iteration(t, par, tt_next, do_tail=True, do_head=True):
                it = t
                pe.wait_ge(bias_ld, (t + 1) * 16)
                pe.wait_ge(rope_done, (t + 1) * 3)
                score(t, 0)
                if do_head:
                    mixing(it, t + 1, tt_next, 1 - par, (0, 1))
                score(t, 1)
                if do_head:
                    mixing(it, t + 1, tt_next, 1 - par, (2, 3))
                turn_probs(t, 0)
                if do_tail:
                    adapter_ranks(it, t - 1)
                if do_head:
                    routing(it)
                if do_tail:
                    hidden_first(it, t - 1)
                attend(t, par, 0)
                turn_probs(t, 1)
                if do_tail:
                    hidden_rest(it)
                if do_head:
                    project(it, "k0", wk)
                    project(it, "k1", wk)
                attend(t, par, 1)
                if do_head:
                    project(it, "q0", wq)
                    project(it, "q1", wq)
                if not do_tail:
                    pe.wait_ge(raw_lo, SPLIT["wo"])
                out_proj(it, t, 0)
                if do_head:
                    project(it, "q2", wq)
                    project(it, "q3", wq)
                turn_rows(it, t, 0)
                out_proj(it, t, 1)
                if do_head:
                    value(it, 0)
                    value(it, 1)
                turn_rows(it, t, 1)

            pe.wait_ge(const_made, 1)
            mixing(AHEAD, 0, 0, 0, range(KC))
            pe.wait_ge(raw_lo, SPLIT["wr"])
            routing(AHEAD)
            pe.wait_ge(raw_lo, SPLIT["wk"])
            for name in ("k0", "k1"):
                project(AHEAD, name, wk)
            pe.wait_ge(raw_lo, SPLIT["wq"])
            for name in ("q0", "q1", "q2", "q3"):
                project(AHEAD, name, wq)
            pe.wait_ge(raw_lo, SPLIT["wv"])
            value(AHEAD, 0)
            value(AHEAD, 1)
            iteration(0, 0, 0, do_tail=False)
            pe.wait_ge(raw_lo, len(RAW))
            with pe.Fori(0, NT // 2 - 1) as n:
                iteration(n * 2 + 1, 1, n + 1)
                iteration(n * 2 + 2, 0, n + 1)
            iteration(NT - 1, 1, 0, do_head=False)
            adapter_ranks(BEHIND, NT - 1)
            hidden_first(BEHIND, NT - 1)
            hidden_rest(BEHIND)

            def gate_up(i, g, pair, j, par, first):
                k, nib_n = j // 2, j % 2
                if j == 0:
                    pe.wait_ge(h_ld[par], (pair + 1) * 16)
                if j % 2 == 0:
                    pe.wait_ge(slot_ld[k], (g + 1) * 16)
                if j >= 2 or not first:
                    pe.wait_ge(inter_done, i * NS + j - 1)
                for m, bank, done in ((0, gate, gate_full), (1, up, up_full)):
                    pairs = [(w_slot[k][:, m, nib, u, c * 256 + nib_n * P:c * 256 + (nib_n + 1) * P], h_in[par][:, 2 * c + nib, v, :])
                             for c in range(2) for nib in range(2) for u, v in THREE]
                    products(bank[j % 2][:], pairs).then_inc(done[j % 2], 1)

            def down_step(i, j, first=False):
                k, nib_n = j // 2, j % 2
                pe.wait_ge(inter_ready, i * NS + j + 1)
                for tc in range(NQ):
                    if j == 0 and not first:
                        pe.wait_ge(acc_added, (i - 1) * NQ + tc + 1)
                    for m, (u, v) in enumerate(THREE):
                        ins = pe.matmul(down[tc][:], inter_parts[:, j % 2, u, tc * P:(tc + 1) * P], w_slot[k][:, 2, nib_n, v, :],
                                        start=(j == 0 and m == 0), stop=(j == NS - 1 and m == 2))
                    if j == NS - 1:
                        ins.then_inc(down_full, 1)
                if j < NS - 1:
                    ins.then_inc(down_done, 1)

            def ffn_tile(g, pair, par, first=False):
                i = pair * 2 + par
                for j in range(NS):
                    gate_up(i, g, pair, j, par, first)
                    if j >= 2:
                        down_step(i, j - 2, first)
                    elif not first:
                        down_step(i - 1, NS - 2 + j)

            NPAIR = NF // 2
            ffn_tile(0, 0, 0, first=True)
            ffn_tile(0, 0, 1)
            with pe.Fori(1, NPAIR) as p:
                ffn_tile(0, p, 0)
                ffn_tile(0, p, 1)
            with pe.Fori(1, NG) as g:
                with pe.Fori(0, NPAIR) as p:
                    ffn_tile(g, g * NPAIR + p, 0)
                    ffn_tile(g, g * NPAIR + p, 1)
            for j in (NS - 2, NS - 1):
                down_step(NG * NF - 1, j)

        @block.scalar
        def _(act):
            act.sem_inc(pT_used, PRIMED)
            def split(j):
                stage, hi, lo = raw_views(j)
                act.wait_ge(raw_ld[j % 2], (j // 2 + 1) * 16)
                act.activation(hi, stage, ACT.Copy).then_inc(raw_hi, 1)

            def mix_diagonal(t, par):
                for b in range(2):
                    rows = slice(b * C, (b + 1) * C)
                    act.activation(mix_tile[rows, par, :, b, :], mix[rows, bass.ds(t * NP, NP), :], ACT.Copy).then_inc(mix_ready, 1)

            def mixed(it, chunks):
                for c in chunks:
                    bank = full_wait(act, it, f"hs{c}")
                    act.activation(hs[:, HI, c, :], bank[:, 0:TOK], ACT.Copy).then_inc(hs_hi, 1)

            def logits(it):
                bank = full_wait(act, it, "z")
                act.activation(z_sb[:], bank[0:HEADS, 0:TOK], ACT.Identity, bias=br[:, 0:1]).then_inc(proj_free[BANK["z"]], 1)

            def rope_bias(it, t, c):
                name = ROPE[c]
                bank = full_wait(act, it, name)
                bias = bk[:, c:c + 1] if c < 2 else bq[:, c - 2:c - 1]
                if c >= 2:
                    act.wait_ge(rope_done, t * 3 + c // 2)
                act.activation(rope_in[:, c % 2, :], bank[:, 0:TOK], ACT.Identity, bias=bias).then_inc(proj_free[BANK[name]], 1)

            def exp(t, q):
                act.wait_ge(scores_used, t * NP + q + 1 + PRIMED)
                act.activation(probs[:, q], probs[:, q], ACT.Exp, scale=ATT_SCALE).then_inc(exp_done, 1)

            def probs_turned(t, q):
                act.wait_ge(pT_full, t * NP + q + 1)
                act.activation(probsT[:], pT[:], ACT.Copy).then_inc(pT_used, 1)

            def heads_high(t, q):
                act.wait_ge(pv_full, t * NP + q + 1)
                act.activation(attnT[:, q, HI].rearrange("p k n -> p (k n)"), pv[:].rearrange("p g r b c -> p (g r b c)"), ACT.Copy).then_inc(pv_hi, 1)

            def rows_high(t, q):
                act.wait_ge(turn_full, t * NP + q + 1)
                act.activation(x1T[:, HI, :, q * P:(q + 1) * P], turn[:], ACT.Copy).then_inc(turn_hi, 1)

            def ranks(it):
                evacuated(act, it, "xa")
                act.activation(xa_parts[:, HI, :], xa[:], ACT.Copy).then_inc(xa_hi, 1)

            def hidden(it, t, n):
                bank = full_wait(act, it, f"h{n}")
                act.wait_ge(h_stored[n % 2], (t * (KC // 2) + n // 2) * 16 + PRIMED)
                act.activation(h_out[:, n % 2, HI, :], bank[:, 0:TOK], ACT.Copy).then_inc(h_hi, 1)

            def iteration(t, par, do_tail=True, do_head=True):
                it = t
                if do_head:
                    mix_diagonal(t + 1, 1 - par)
                    mixed(it, (0, 1))
                exp(t, 0)
                if do_head:
                    mixed(it, (2, 3))
                probs_turned(t, 0)
                exp(t, 1)
                if do_tail:
                    ranks(it)
                if do_head:
                    logits(it)
                if do_tail:
                    hidden(it, t - 1, 0)
                    hidden(it, t - 1, 1)
                heads_high(t, 0)
                probs_turned(t, 1)
                if do_tail:
                    hidden(it, t - 1, 2)
                    hidden(it, t - 1, 3)
                if do_head:
                    rope_bias(it, t + 1, 0)
                    rope_bias(it, t + 1, 1)
                heads_high(t, 1)
                if do_head:
                    for c in range(2, 6):
                        rope_bias(it, t + 1, c)
                rows_high(t, 0)
                rows_high(t, 1)

            act.wait_ge(mix_cleared, 1)
            act.wait_ge(gather_first, NP * 16)
            mix_diagonal(0, 0)
            split(0)
            split(1)
            mixed(AHEAD, range(KC))
            act.wait_ge(const_ld, N_CONST * 16)
            logits(AHEAD)
            split(2)
            rope_bias(AHEAD, 0, 0)
            rope_bias(AHEAD, 0, 1)
            split(3)
            for c in range(2, 6):
                rope_bias(AHEAD, 0, c)
            for j in range(4, len(RAW)):
                split(j)
            act.wait_ge(gather_rest, (B // 2 - NP) * 16)
            iteration(0, 0, do_tail=False)
            with act.Fori(0, NT // 2 - 1) as n:
                iteration(n * 2 + 1, 1)
                iteration(n * 2 + 2, 0)
            iteration(NT - 1, 1, do_head=False)
            ranks(BEHIND)
            for n in range(KC):
                hidden(BEHIND, NT - 1, n)

            def ffn_tile(i, first=False):
                for j in range(NS):
                    b = j % 2
                    n = i * (NS // 2) + j // 2
                    act.wait_ge(gate_full[b], n + 1)
                    act.activation(gate_sq[:], gate[b][:], ACT.Square).then_inc(sq_done, 1)
                    act.wait_ge(gin_done, i * NS + j + 1)
                    act.activation(gate_tanh[:], gate_in[:], ACT.Tanh, scale=GELU_SCALE * GELU_CUBIC).then_inc(tanh_done, 1)
                    if not (first and j < 2):
                        if j == 1:
                            act.wait_ge(down_full, i * NQ)
                        else:
                            act.wait_ge(down_done, i * (NS - 1) + max(j - 1, 0))
                    act.wait_ge(inter_done, i * NS + j + 1)
                    act.activation(inter_parts[:, b, HI, :], inter[:], ACT.Copy).then_inc(inter_hi, 1)

            ffn_tile(0, first=True)
            with act.Fori(1, NG * NF) as i:
                ffn_tile(i)

        @block.vector
        def _(dve):
            for q in (*proj_free, scores_used, pv_used, turn_used):
                dve.sem_inc(q, PRIMED)

            def passed():
                dve.sem_inc(dve_passed, 1)

            dve.wait_ge(index_ld, 48)
            dve.tensor_scalar(cond_row[:], cond_of[:], float(C), columns[:, 0:1], ALU.mult, ALU.add).then_inc(cond_row_ready, 1)
            dve.memset(mix_tile[:], 0.0).then_inc(mix_cleared, 1)

            def dequantise(c, k):
                m, nib = k // 2, k % 2
                base = c * 36 + 6 * k
                if nib == 0:
                    dve.wait_ge(packed_ld[m], (c + 1) * (48 if m < 2 else 32))
                if k >= 2:
                    dve.wait_ge(w_step, c * 12 + 2 * k - 2 + PRIMED)
                elif k == 0:
                    dve.wait_ge(w_step, c * 12 + PRIMED)
                dve.tensor_scalar(magnitude[:], packed[:, m, :], 4 * nib, 7, ALU.logical_shift_right, ALU.bitwise_and).then_inc(dq_step, 1)
                dve.tensor_scalar(signed_scale[:, k % 2, :], packed[:, m, :], 28 - 4 * nib, -2 ** 31, ALU.logical_shift_left, ALU.bitwise_and).then_inc(dq_step, 1)
                dve.wait_ge(dq_step, base + 1)
                dve.tensor_scalar(lut_line[:], magnitude[:], 2.0, -8.0, ALU.mult, ALU.add).then_inc(dq_step, 1)
                dve.wait_ge(dq_step, base + 2)
                dve.tensor_tensor(signed_scale[:, k % 2, :], signed_scale[:, k % 2, :], scales[:, m, :].bitcast(I32), ALU.bitwise_xor).then_inc(dq_step, 1)
                dve.wait_ge(dq_step, base + 3)
                dve.scalar_tensor_tensor(lut_line[:], magnitude[:], -2.0, lut_line[:], ALU.add, ALU.max).then_inc(dq_step, 1)
                dve.wait_ge(dq_step, base + 5)
                dve.scalar_tensor_tensor(lut_v[:, k % 2, :], magnitude[:], 0.5, lut_line[:], ALU.mult, ALU.max).then_inc(dq_step, 1)

            def split(j):
                stage, hi, lo = raw_views(j)
                dve.wait_ge(raw_hi, j + 1)
                dve.tensor_tensor(lo, stage, hi.bitcast(F32), ALU.subtract).then_inc(raw_lo, 1)

            def mixed(t, chunks):
                for c in chunks:
                    name = f"hs{c}"
                    dve.wait_ge(hs_hi, t * KC + c + 1)
                    dve.tensor_tensor(hs[:, LO, c, :], proj[BANK[name]][:, 0:TOK], hs[:, HI, c, :].bitcast(F32), ALU.subtract) \
                       .then_inc(proj_free[BANK[name]], 1)

            def rope(it, t, n):
                def by_position(buf):
                    return buf[:].rearrange("p k (b c) -> p (k b) c", c=C)

                s0 = (t * 3 + n) * 3
                for c in (2 * n, 2 * n + 1):
                    evacuated(dve, it, ROPE[c])
                    passed()
                dve.stream_shuffle(rope_sin[:], rope_in[:], [(i + HD // 2) % HD for i in range(HD)]).then_inc(rope_step, 1)
                dve.wait_ge(rope_step, s0 + 1)
                dve.tensor_tensor(by_position(rope_in), by_position(rope_in), cos[:].unsqueeze(1).to_broadcast([P, 2 * NB, C]), ALU.mult).then_inc(rope_step, 1)
                dve.tensor_tensor(by_position(rope_sin), by_position(rope_sin), sin[:].unsqueeze(1).to_broadcast([P, 2 * NB, C]), ALU.mult).then_inc(rope_step, 1)
                dve.wait_ge(rope_step, s0 + 3)
                dst = kT[:].rearrange("p k (b c) -> p k b c", c=C) if n == 0 else qT[:, n - 1].rearrange("p b r c -> p r b c")
                dve.tensor_tensor(dst, *(buf[:].rearrange("p k (b c) -> p k b c", c=C) for buf in (rope_in, rope_sin)), ALU.add).then_inc(rope_done, 1)

            def top_keys(t):
                steps = 2 * TOPK // 8 + 1
                s0 = t * steps
                dve.wait_ge(z_ld, (t + 1) * 16)
                dve.tensor_scalar(rank[:], z_rows[:], SIGMOID_ONE, SIGMOID_ZERO, ALU.min, ALU.max).then_inc(topk_step, 1)
                for r in range(TOPK // 8):
                    dve.wait_ge(topk_step, s0 + 2 * r + 1)
                    passed()
                    dve.max(top8[:], rank[:]).then_inc(topk_step, 1)
                    dve.wait_ge(topk_step, s0 + 2 * r + 2)
                    passed()
                    dve.match_replace(rank[:], top8[:], rank[:], PICKED).then_inc(topk_step, 1)
                dve.wait_ge(topk_step, s0 + steps)
                dve.tensor_scalar(key_bias[:], rank[:], PICKED / 2, MASKED, ALU.is_gt, ALU.mult).then_inc(bias_ready, 1)

            def value(it, par, q):
                bank = full_wait(dve, it, f"v{q}")
                dve.tensor_tensor(v_sb[:, par, q].rearrange("p g d -> p (g d)"), bank[:, 0:256], bv[:], ALU.add).then_inc(proj_free[BANK[f"v{q}"]], 1)

            def softmax_shift(t, q):
                dve.wait_ge(score_step, (t * NP + q) * 8 + 8)
                dve.tensor_reduce(row_max[:, q], scores[:], AX_X, ALU.max).then_inc(scores_max, 1)
                dve.wait_ge(scores_max, t * NP + q + 1)
                dve.tensor_tensor(probs[:, q].rearrange("p g b c -> p b g c"), scores[:],
                                  row_max[:, q].unsqueeze(3).to_broadcast([P, 2, KV_HEADS, C]), ALU.subtract).then_inc(scores_used, 1)

            def softmax_sum(t, q):
                dve.wait_ge(exp_done, t * NP + q + 1)
                dve.tensor_reduce(row_sum[:, q], probs[:, q].rearrange("p g b c -> p b g c"), AX_X, ALU.add).then_inc(sum_step, 1)
                dve.wait_ge(sum_step, (t * NP + q) * 2 + 1)
                dve.reciprocal(row_inv[:, q], row_sum[:, q]).then_inc(sum_step, 1)

            def normalise(t, q):
                dve.wait_ge(sum_step, (t * NP + q) * 2 + 2)
                pr = probs[:, q].rearrange("p g b c -> p b g c")
                dve.tensor_tensor(pr, pr, row_inv[:, q].unsqueeze(3).to_broadcast([P, 2, KV_HEADS, C]), ALU.mult).then_inc(probs_ready, 1)

            def heads_low(t, q):
                dve.wait_ge(pv_hi, t * NP + q + 1)
                dve.tensor_tensor(attnT[:, q, LO].rearrange("p k n -> p (k n)"), pv[:].rearrange("p g r b c -> p (g r b c)"),
                                  attnT[:, q, HI].rearrange("p k n -> p (k n)").bitcast(F32), ALU.subtract).then_inc(pv_used, 1)

            def rows_low(t, q):
                dve.wait_ge(turn_hi, t * NP + q + 1)
                hi, lo = (x1T[:, u, :, q * P:(q + 1) * P] for u in (HI, LO))
                dve.tensor_tensor(lo, turn[:], hi.bitcast(F32), ALU.subtract).then_inc(turn_used, 1)

            def add_residual(it, t, q):
                bank = full_wait(dve, it, f"o{q}")
                if q == 0:
                    dve.wait_ge(residual_ready, t + 1)
                dve.tensor_tensor(x1[:, q, :], bank[:], x1[:, q, :], ALU.add).then_inc(proj_free[BANK[f"o{q}"]], 1)

            def mask_ranks(it, t):
                bank = full_wait(dve, it, "xa")
                dve.tensor_tensor(xa[:].rearrange("p (b c) -> p b c", c=C), bank[:, 0:TOK].rearrange("p (b c) -> p b c", c=C),
                                  adapter_mask[:, bass.ds(t * NB, NB)].unsqueeze(2).to_broadcast([P, NB, C]), ALU.mult).then_inc(proj_free[BANK["xa"]], 1)

            def ranks_low(t):
                dve.wait_ge(xa_hi, t + 1)
                dve.tensor_tensor(xa_parts[:, LO, :], xa[:], xa_parts[:, HI, :].bitcast(F32), ALU.subtract).then_inc(xa_lo, 1)

            def hidden(t, n):
                dve.wait_ge(h_hi, t * KC + n + 1)
                dve.tensor_tensor(h_out[:, n % 2, LO, :], proj[BANK[f"h{n}"]][:, 0:TOK], h_out[:, n % 2, HI, :].bitcast(F32), ALU.subtract) \
                   .then_inc(proj_free[BANK[f"h{n}"]], 1)

            def iteration(t, par, c, k0, do_tail=True, do_head=True):
                it = t
                softmax_shift(t, 0)
                if do_head:
                    mixed(t + 1, (0, 1))
                softmax_sum(t, 0)
                normalise(t, 0)
                if do_head:
                    mixed(t + 1, (2, 3))
                softmax_shift(t, 1)
                if do_tail:
                    mask_ranks(it, t - 1)
                softmax_sum(t, 1)
                if do_tail:
                    ranks_low(t - 1)
                normalise(t, 1)
                if do_tail:
                    hidden(t - 1, 0)
                    hidden(t - 1, 1)
                dequantise(c, k0)
                heads_low(t, 0)
                if do_tail:
                    hidden(t - 1, 2)
                    hidden(t - 1, 3)
                if do_head:
                    rope(it, t + 1, 0)
                    top_keys(t + 1)
                heads_low(t, 1)
                if do_head:
                    rope(it, t + 1, 1)
                add_residual(it, t, 0)
                dequantise(c, k0 + 1)
                if do_head:
                    rope(it, t + 1, 2)
                rows_low(t, 0)
                add_residual(it, t, 1)
                if do_head:
                    value(it, 1 - par, 0)
                    value(it, 1 - par, 1)
                rows_low(t, 1)
                dequantise(c, k0 + 2)

            split(0)
            split(1)
            dve.wait_ge(const_ld, N_CONST * 16)
            dve.tensor_copy(batch_rows[:], batch_rows_f[:])
            dve.tensor_scalar(adapter_mask[:], adapter_of[:], columns[:, 1:2], adapter_scale[:, 0:1],
                              ALU.is_equal, ALU.mult).then_inc(const_made, 1)
            mixed(0, range(KC))
            split(2)
            rope(AHEAD, 0, 0)
            split(3)
            top_keys(0)
            rope(AHEAD, 0, 1)
            rope(AHEAD, 0, 2)
            value(AHEAD, 0, 0)
            value(AHEAD, 0, 1)
            for j in range(4, len(RAW)):
                split(j)
            iteration(0, 0, 0, 0, do_tail=False)
            with dve.Fori(0, NT // 2 - 1) as n:
                iteration(n * 2 + 1, 1, n, 3)
                iteration(n * 2 + 2, 0, n + 1, 0)
            iteration(NT - 1, 1, NT // 2 - 1, 3, do_head=False)
            mask_ranks(BEHIND, NT - 1)
            ranks_low(NT - 1)
            for n in range(KC):
                hidden(NT - 1, n)

            def add_down(i, pair, par):
                dve.wait_ge(acc_ld[par], (pair + 1) * 16)
                for tc in range(NQ):
                    dve.wait_ge(down_full, i * NQ + tc + 1)
                    dve.tensor_tensor(acc[par][:, tc, :], down[tc][:], acc[par][:, tc, :], ALU.add).then_inc(acc_added, 1)

            def ffn_tile(pair, par, first=False, block_c=None):
                i = pair * 2 + par
                for j in range(NS):
                    b = j % 2
                    n = i * NS + j + 1
                    dve.wait_ge(sq_done, n)
                    dve.scalar_tensor_tensor(gate_in[:], gate_sq[:], 1.0 / GELU_CUBIC, gate[b][:], ALU.add, ALU.mult).then_inc(gin_done, 1)
                    if block_c is not None and j < 6:
                        dequantise(block_c, j)
                    if j == 2 and not first:
                        add_down(i - 1, pair - 1 if par == 0 else pair, 1 - par)
                    dve.wait_ge(tanh_done, n)
                    dve.scalar_tensor_tensor(gate_val[:], gate_tanh[:], 1.0, gate[b][:], ALU.add, ALU.mult).then_inc(gval_done, 1)
                    dve.wait_ge(gval_done, n)
                    dve.wait_ge(up_full[b], i * (NS // 2) + j // 2 + 1)
                    dve.scalar_tensor_tensor(inter[:], gate_val[:], 0.5, up[b][:], ALU.mult, ALU.mult).then_inc(inter_done, 1)
                    dve.wait_ge(inter_hi, n)
                    dve.tensor_tensor(inter_parts[:, b, LO, :], inter[:], inter_parts[:, b, HI, :].bitcast(F32), ALU.subtract).then_inc(inter_ready, 1)

            NPAIR = NF // 2
            ffn_tile(0, 0, first=True, block_c=NF)
            ffn_tile(0, 1, block_c=NF + 1)
            with dve.Fori(1, NPAIR) as p:
                ffn_tile(p, 0, block_c=p * 2 + NF)
                ffn_tile(p, 1, block_c=p * 2 + NF + 1)
            with dve.Fori(NPAIR, NG * NPAIR) as p:
                ffn_tile(p, 0)
                ffn_tile(p, 1)
            add_down(NG * NF - 1, NG * NPAIR - 1, 1)


def rope_tables(C):
    inv_freq = (1.0 / ROPE_THETA ** (np.arange(0, HD, 2, dtype=np.float32) / HD)).astype(np.float32)
    freqs = np.arange(C, dtype=np.float32)[:, None] * inv_freq[None, :]
    emb = np.concatenate([freqs, freqs], axis=-1)
    cos, sin = np.cos(emb).astype(np.float32), np.sin(emb).astype(np.float32)
    sin = np.concatenate([-sin[:, :HD // 2], sin[:, HD // 2:]], axis=-1)
    return np.ascontiguousarray(np.tile(cos.T, (4, 1))), np.ascontiguousarray(np.tile(sin.T, (4, 1)))


def kernel(**inputs):
    import numpy as np
    import concourse.bacc as bacc
    from concourse import mybir
    from concourse.bass_utils import run_bass_kernel_spmd

    def get(name):
        return np.asarray(inputs[name])

    x = get("x")
    B, C, D = x.shape
    MLP = get("L0_ffn_gate_W_packed").shape[0]
    NCP = MLP // 256
    NB = TOK // C

    def head_order(w):
        lead = w.shape[:-1]
        w = w.reshape(*lead, 2, 4, 2, HD)
        return np.moveaxis(w, -2, -3).reshape(*lead, HEADS * HD)

    def repeat_major(w):
        return np.swapaxes(w.reshape(*w.shape[:-1], KV_HEADS, 2), -1, -2).reshape(w.shape)

    def nibble_order(w):
        lead = w.shape[:-1]
        return np.swapaxes(w.reshape(*lead, 2, P, 2), -1, -2).reshape(*lead, D)

    def channel_order(w):
        r = w.shape[0]
        return w.reshape(r, NCP, P, 2).transpose(1, 0, 3, 2).reshape(NCP, r, 256)

    def gate_pack(w):
        return channel_order(w.T).reshape(NCP, 2, P, 256).transpose(0, 2, 1, 3).reshape(NCP, P, 512)

    cos, sin = rope_tables(C)
    batch_rows = np.zeros((NB, 2, NB, 2, C), np.float32)
    for b in range(NB):
        for r in range(2):
            batch_rows[b, r, b, r] = 1.0
    batch_rows = batch_rows.reshape(2 * NB, NB, P)
    columns = np.stack([np.arange(P) % C, np.arange(P) // RANK], axis=1).astype(np.float32)
    arrays = {
        "x": x,
        "cond_index": get("itok_B_1_198").reshape(B // 2, 2).T,
        "adapter_index": get("itok_B_0_6")[None, :],
        "cond_weights": get("L0_cond_weights"),
        "wq": head_order(get("L0_attn_Wq")),
        "bq": head_order(get("L0_attn_bq")).reshape(4, P).T,
        "wk": get("L0_attn_Wk"),
        "bk": get("L0_attn_bk").reshape(2, P).T,
        "wv": get("L0_attn_Wv"),
        "bv": get("L0_attn_bv")[None, :],
        "wo": head_order(get("L0_attn_Wo").T).T,
        "bo": get("L0_attn_bo")[None, :],
        "wr": repeat_major(get("L0_attn_Wr")),
        "br": repeat_major(get("L0_attn_br"))[:, None],
        "w2": nibble_order(get("L0_cond2_W").T),
        "wa": get("L0_cond2_A").reshape(ADAPTERS * RANK, D).T,
        "wb": nibble_order(get("L0_cond2_Bm").transpose(0, 2, 1).reshape(ADAPTERS * RANK, D)),
        "adapter_scales": np.repeat(get("L0_cond2_scalings"), RANK)[:, None],
        "gate_packed": gate_pack(get("L0_ffn_gate_W_packed")),
        "gate_scales": channel_order(get("L0_ffn_gate_scales").T),
        "up_packed": gate_pack(get("L0_ffn_up_W_packed")),
        "up_scales": channel_order(get("L0_ffn_up_scales").T),
        "down_packed": get("L0_ffn_down_W_packed").T.reshape(NCP, P, D),
        "down_scales": get("L0_ffn_down_scales").T.reshape(NCP, 8, D),
        "cos": cos, "sin": sin,
        "identity": np.eye(P, dtype=np.float32),
        "batch_rows": batch_rows,
        "columns": columns,
    }
    nc = bacc.Bacc("TRN2", target_bir_lowering=False, num_devices=1)
    given, aps = {}, {}
    for name, v in arrays.items():
        v = np.ascontiguousarray(v)
        given["in_" + name] = v
        aps[name] = nc.dram_tensor("in_" + name, v.shape, mybir.dt.from_np(v.dtype), kind="ExternalInput").ap()
    out = nc.dram_tensor("out_0", (B, C, D), mybir.dt.float32, kind="ExternalOutput").ap()
    build(nc, aps, out)
    r = run_bass_kernel_spmd(nc, [given], core_ids=[0])
    return r.results[0]["out_0"]
```

```python
from contextlib import ExitStack

import numpy as np

import concourse.bass as bass
from concourse import mybir

F32 = mybir.dt.float32
F32R = mybir.dt.float32r
I32 = mybir.dt.int32
U32 = mybir.dt.uint32
BF16 = mybir.dt.bfloat16
ALU = mybir.AluOpType
ACT = mybir.ActivationFunctionType
AX_X = mybir.AxisListType.X

P = 128
HEADS, KV_HEADS, HD = 16, 8, 32
ROPE_THETA = 1000000.0
RANK, ADAPTERS = 16, 8
TOK = 256
TILE = 512
SIGMOID_ONE = 24 * float(np.log(2.0))
SIGMOID_ZERO = -88.72
PICKED = -1.0e30
MASKED = -1.0e30
GELU_CUBIC = 0.044715
GELU_SCALE = 0.7978845608028654
HI, LO = 0, 1
THREE = [(HI, HI), (HI, LO), (LO, HI)]


def build(nc, a, out):
    B, C, D = a["x"].shape
    NCP = a["gate_packed"].shape[0]
    KC = D // P
    NB = TOK // C
    NP = NB // 2
    NT = B // NB
    NF = B * C // TILE
    NQ = TILE // P
    GB = 4
    NG = NCP // GB
    NS = 2 * GB
    TOPK = C // 2
    assert D == TILE and C == 64 and NG > 2 and NT % 2 == 0 and NF >= 4 and NCP == 2 * NF and NT == 2 * NF
    ATT_SCALE = HD ** -0.5

    h_scr = nc.dram_tensor("h_scratch", (NF, P, KC, 2, TILE), F32, kind="Internal").ap()
    w_scr = nc.dram_tensor("w_scratch", (NCP, P, 3, 2, 2, 512), F32, kind="Internal").ap()
    z_scr = nc.dram_tensor("z_scratch", (NT, NB, HEADS, C), F32, kind="Internal").ap()
    m_scr = nc.dram_tensor("m_scratch", (NT, NB, HEADS, C), BF16, kind="Internal").ap()

    x_v = a["x"].rearrange("(t q b) c d -> t (b c) q d", q=NP, b=2)
    x1_v = out.rearrange("(t q b) c d -> t (b c) q d", q=NP, b=2)
    out_tiles = out.rearrange("(t q b) c d -> t (b c) q d", q=NQ, b=2)
    cond_rows = a["cond_weights"].rearrange("s c d -> (s c) d")

    with ExitStack() as ctx:
        def sem(name):
            return ctx.enter_context(nc.semaphore(name))

        def sb_in(stack):
            return lambda name, shape, dt: stack.enter_context(nc.sbuf_tensor(name, shape, dt))

        def ps_in(stack):
            return lambda name, shape, dt: stack.enter_context(nc.psum_tensor(name, shape, dt))

        sb = sb_in(ctx)
        packed = sb("packed", [P, 3, 512], I32)
        scales = sb("scales", [P, 3, 512], F32)
        magnitude = sb("magnitude", [P, 512], I32)
        signed_scale = sb("signed_scale", [P, 2, 512], I32)
        lut_line = sb("lut_line", [P, 512], F32)
        lut_v = sb("lut_v", [P, 2, 512], F32)
        w_parts = sb("w_parts", [P, 2, 2, 512], F32R)

        with ExitStack() as token_stage:
            sb = sb_in(token_stage)
            ps = ps_in(token_stage)
            wq = sb("wq", [P, 2, KC, 512], F32R)
            wk = sb("wk", [P, 2, KC, 256], F32R)
            wv = sb("wv", [P, 2, KC, 256], F32R)
            wo = sb("wo", [P, 2, KC, 512], F32R)
            k_diagonal = sb("k_diagonal", [P, 2, NB, 2, 4, C], F32R)
            w2 = sb("w2", [P, 2, KC, 512], F32R)
            wr = sb("wr", [P, 2, KC, HEADS], F32R)
            wa = sb("wa", [P, 2, KC, P], F32R)
            wb = sb("wb", [P, 2, 512], F32R)
            bq = sb("bq", [P, 4], F32)
            bk = sb("bk", [P, 2], F32)
            bv = sb("bv", [P, 256], F32)
            bo = sb("bo", [P, 512], F32)
            br = sb("br", [HEADS, 1], F32)
            cos = sb("cos", [P, C], F32)
            sin = sb("sin", [P, C], F32)
            identity = sb("identity", [P, P], F32)
            batch_rows = sb("batch_rows", [2 * NB, NB, P], BF16)
            columns = sb("columns", [P, 2], F32)
            adapter_of = sb("adapter_of", [P, B], I32)
            adapter_scale = sb("adapter_scale", [P, 1], F32)
            adapter_mask = sb("adapter_mask", [P, B], F32)
            cond_of = sb("cond_of", [P, B // 2], I32)
            cond_row = sb("cond_row", [P, B // 2], U32)
            mix = sb("mix", [P, B // 2, C], F32)
            mix_tile = sb("mix_tile", [P, 2, NP, 2, C], F32)
            x_in = sb("x_in", [P, 2, NP, D], F32)
            x1 = sb("x1", [P, NP, D], F32)
            hs = sb("hs", [P, 2, KC, TOK], F32R)
            z_rows = sb("z_rows", [NB * HEADS, C], F32)
            rank = sb("rank", [NB * HEADS, C], F32)
            top8 = sb("top8", [NB * HEADS, 8], F32)
            key_bias = sb("key_bias", [NB * HEADS, C], BF16)
            bias_rows = sb("bias_rows", [2 * NB, KV_HEADS * C], BF16)
            rope_in = sb("rope_in", [P, 2, 2, TOK], F32)
            rope_sin = sb("rope_sin", [P, 2, TOK], F32)
            q_parts = sb("q_parts", [P, 2, 2, NB, 2, C], F32R)
            v_sb = sb("v_sb", [P, NP, KV_HEADS, HD], F32)
            with ExitStack() as staging:
                w_stage = sb_in(staging)("w_stage", [P, 2, KC, 512], F32)
                wa_stage = sb_in(staging)("wa_stage", [P, KC, P], F32)
                wb_stage = sb_in(staging)("wb_stage", [P, D], F32)
                batch_rows_f = sb_in(staging)("batch_rows_f", [2 * NB, NB, P], F32)
            probs = sb("probs", [P, NP, KV_HEADS, 2, C], F32)
            probsT = sb("probsT", [P, KV_HEADS, P], F32)
            attnT = sb("attnT", [P, 2, KC, P], F32R)
            row_max = sb("row_max", [P, NP, 2, KV_HEADS], F32)
            row_sum = sb("row_sum", [P, NP, 2, KV_HEADS], F32)
            row_inv = sb("row_inv", [P, NP, 2, KV_HEADS], F32)
            x1T = sb("x1T", [P, 2, KC, TOK], F32R)
            xa = sb("xa", [P, TOK], F32)
            z_sb = xa[0:HEADS, :]
            k_whole = sb("k_whole", [P, 2, TOK], F32R)
            xa_parts = sb("xa_parts", [P, 2, TOK], F32R)
            h_out = sb("h_out", [P, 2, 2, TOK], F32R)
            proj = [ps(f"proj{i}", [P, 512], F32) for i in range(2)]
            scores = [ps(f"scores{q}", [P, 2, KV_HEADS, C], F32) for q in range(NP)]
            pT = [bank[:].rearrange("p b (h e) c -> p (b h) (e c)", e=2) for bank in scores]
            pv = ps("pv", [P, 2, 2, 2, C], F32)
            turn = ps("turn", [P, KC, P], F32)

        with ExitStack() as ffn_stage:
            sb = sb_in(ffn_stage)
            ps = ps_in(ffn_stage)
            def weight_slot(k):
                return sb(f"w_slot{k}", [P, 3, 2, 2, 512], F32R)

            def tile_in(k):
                return sb(f"h_in{k}", [P, KC, 2, TILE], F32R)

            first_slots = [weight_slot(0), weight_slot(1)]
            first_tile = tile_in(0)
            w_slot = first_slots + [weight_slot(k) for k in range(2, GB)]
            h_in = [first_tile, tile_in(1)]
            acc = [sb(f"acc{k}", [P, NQ, D], F32) for k in range(2)]
            gate_sq = sb("gate_sq", [P, TILE], F32)
            gate_in = sb("gate_in", [P, TILE], F32)
            gate_tanh = sb("gate_tanh", [P, TILE], F32)
            gate_val = sb("gate_val", [P, TILE], F32)
            inter = sb("inter", [P, TILE], F32)
            inter_parts = sb("inter_parts", [P, 2, 2, TILE], F32R)
            down = [ps(f"down{i}", [P, D], F32) for i in range(NQ)]
            gate = [ps(f"gate{i}", [P, TILE], F32) for i in range(2)]
            up = [ps(f"up{i}", [P, TILE], F32) for i in range(2)]

        index_ld = sem("index_ld")
        const_ld = sem("const_ld")
        const_made = sem("const_made")
        cond_row_ready = sem("cond_row_ready")
        gather_first, gather_second, gather_rest = sem("gather_first"), sem("gather_second"), sem("gather_rest")
        raw_ld = [sem(f"raw_ld{n}") for n in range(4)]
        raw_hi, raw_lo = sem("raw_hi"), sem("raw_lo")
        mix_cleared, mix_ready = sem("mix_cleared"), sem("mix_ready")
        scores_full, pv_step = sem("scores_full"), sem("pv_step")
        x_ld = [sem("x_ld0"), sem("x_ld1")]
        proj_full = [sem("proj_full0"), sem("proj_full1")]
        proj_free = [sem("proj_free0"), sem("proj_free1")]
        hs_hi = sem("hs_hi")
        z_stored, z_ld = sem("z_stored"), sem("z_ld")
        topk_step, bias_ready, bias_stored, bias_ld = sem("topk_step"), sem("bias_ready"), sem("bias_stored"), sem("bias_ld")
        rope_step, rope_done = sem("rope_step"), sem("rope_done")
        k_cleared, k_hi, k_lo, k_ready = sem("k_cleared"), sem("k_hi"), sem("k_lo"), sem("k_ready")
        q_hi, q_ready = sem("q_hi"), [sem("q_ready0"), sem("q_ready1")]
        scores_max, scores_used = sem("scores_max"), sem("scores_used")
        exp_done, sum_step, probs_ready = sem("exp_done"), sem("sum_step"), sem("probs_ready")
        pT_full, pT_used = sem("pT_full"), sem("pT_used")
        pv_full, pv_hi, pv_used = sem("pv_full"), sem("pv_hi"), sem("pv_used")
        turn_full, turn_hi, turn_used = sem("turn_full"), sem("turn_hi"), sem("turn_used")
        residual_ready, x1_stored = sem("residual_ready"), sem("x1_stored")
        xa_hi, xa_lo = sem("xa_hi"), sem("xa_lo")
        h_hi = sem("h_hi")
        h_stored = [sem("h_stored0"), sem("h_stored1")]
        packed_ld = [sem(f"packed_ld{m}") for m in range(3)]
        dq_step, w_used, w_step = sem("dq_step"), sem("w_used"), sem("w_step")
        w_stored = [sem("w_stored0"), sem("w_stored1")]
        pool_passed = sem("pool_passed")
        dve_passed = sem("dve_passed")
        pe_passed = sem("pe_passed")
        sp_passed = sem("sp_passed")
        slot_ld = [sem(f"slot_ld{k}") for k in range(GB)]
        h_ld = [sem("h_ld0"), sem("h_ld1")]
        acc_ld = [sem("acc_ld0"), sem("acc_ld1")]
        acc_stored = [sem("acc_stored0"), sem("acc_stored1")]
        gate_full = [sem("gate_full0"), sem("gate_full1")]
        up_full = [sem("up_full0"), sem("up_full1")]
        down_done, down_full, acc_added = sem("down_done"), sem("down_full"), sem("acc_added")
        sq_done, gin_done, tanh_done, gval_done = sem("sq_done"), sem("gin_done"), sem("tanh_done"), sem("gval_done")
        inter_done, inter_hi, inter_ready = sem("inter_done"), sem("inter_hi"), sem("inter_ready")

        TAIL = ["xa", "h0", "h1", "h2", "h3"]
        BODY = ["v0", "v1", "o0", "o1"]
        HEAD = ["hs0", "hs1", "hs2", "hs3", "z", "k0", "k1", "q0", "q1", "q2", "q3"]
        USES = ["v0", "v1", "xa", "h0", "h1", "hs0", "hs1", "hs2", "hs3", "z", "k0", "k1", "h2", "h3", "o0",
                "q0", "q1", "q2", "q3", "o1"]
        BANK = {name: n % 2 for n, name in enumerate(USES)}
        ROPE = ("k0", "k1", "q0", "q1", "q2", "q3")

        PRIMED = 1
        AHEAD, BEHIND = "ahead", "behind"

        def uses_before(it, name):
            bank = BANK[name]

            def count(names):
                return sum(BANK[x] == bank for x in names)

            if isinstance(it, str) and it == AHEAD:
                return count(HEAD[:HEAD.index(name)])
            before = USES[:USES.index(name)]
            if isinstance(it, int) and it == 0:
                return count(HEAD) + count([x for x in before if x not in TAIL])
            start = count(HEAD) - count(TAIL)
            if isinstance(it, str) and it == BEHIND:
                return start + (NT - 1) * count(USES) + count(TAIL) + count(BODY) + count(TAIL[:TAIL.index(name)])
            if isinstance(it, int) and it == NT - 1:
                return start + it * count(USES) + count([x for x in before if x not in HEAD])
            return start + it * count(USES) + count(before)

        def full_wait(eng, it, name):
            eng.wait_ge(proj_full[BANK[name]], uses_before(it, name) + 1)
            return proj[BANK[name]]

        def evacuated(eng, it, name):
            eng.wait_ge(proj_free[BANK[name]], uses_before(it, name) + 1 + PRIMED)

        RAW = [("wr", wr, HEADS, 0), ("wk", wk, 256, 1), ("wa", wa, P, 2), ("wb", wb, None, 3),
               ("wq", wq, 512, 0), ("wv", wv, 256, 1), ("wo", wo, 512, 0), ("w2", w2, 512, 1)]
        SPLIT = {name: j + 1 for j, (name, *_) in enumerate(RAW)}
        N_CONST = 11
        stages = [w_stage[:, 0], w_stage[:, 1], wa_stage, wb_stage]

        def stage_uses(j):
            return [i for i in range(j) if RAW[i][3] == RAW[j][3]]

        def raw_views(j):
            _, parts, cols, n = RAW[j]
            if cols is None:
                return stages[n][:], parts[:, HI, :], parts[:, LO, :]
            return stages[n][:, :, 0:cols], parts[:, HI], parts[:, LO]

        block = ctx.enter_context(nc.Block())

        @block.sync
        def _(sp):
            for q in (*h_stored, x1_stored):
                sp.sem_inc(q, PRIMED)

            def passed():
                sp.sem_inc(sp_passed, 1)

            sp.dma_start(cond_of[0:C, :], a["cond_index"][0:1, :].to_broadcast([C, B // 2])).then_inc(index_ld, 16)
            sp.dma_start(cond_of[C:P, :], a["cond_index"][1:2, :].to_broadcast([C, B // 2])).then_inc(index_ld, 16)
            sp.dma_start(columns[:], a["columns"]).then_inc(index_ld, 16)
            sp.dma_start(x_in[:, 0], x_v[0]).then_inc(x_ld[0], 16)

            def load_raw(j):
                name, _, cols, n = RAW[j]
                if stage_uses(j):
                    sp.wait_ge(raw_lo, stage_uses(j)[-1] + 1)
                sp.dma_start(raw_views(j)[0], a[name] if cols is None else a[name].rearrange("(k p) n -> p k n", p=P)).then_inc(raw_ld[n], 16)

            for j in range(4):
                load_raw(j)
            for dst, src in ((bq, a["bq"]), (bk, a["bk"]), (cos, a["cos"]), (sin, a["sin"]),
                             (identity, a["identity"]), (batch_rows_f, a["batch_rows"]), (br, a["br"])):
                sp.dma_start(dst[:], src).then_inc(const_ld, 16)
            sp.dma_start(bv[:], a["bv"].to_broadcast([P, 256])).then_inc(const_ld, 16)
            sp.dma_start(bo[:], a["bo"].to_broadcast([P, 512])).then_inc(const_ld, 16)
            sp.dma_start(adapter_of[:], a["adapter_index"].to_broadcast([P, B])).then_inc(const_ld, 16)
            sp.dma_start(adapter_scale[:], a["adapter_scales"]).then_inc(const_ld, 16)
            load_raw(SPLIT["wq"] - 1)
            load_raw(SPLIT["wv"] - 1)
            sp.dma_start(x_in[:, 1], x_v[1]).then_inc(x_ld[1], 16)

            def route(it, t):
                evacuated(sp, it, "z")
                passed()
                sp.dma_start(z_scr[t].rearrange("b h c -> h b c"), z_sb.rearrange("h (b c) -> h b c", c=C)).then_inc(z_stored, 16)
                sp.wait_ge(z_stored, (t + 1) * 16)
                passed()
                sp.dma_start(z_rows[:], z_scr[t].rearrange("b h c -> (b h) c")).then_inc(z_ld, 16)

            def bias(t):
                sp.wait_ge(bias_ready, t + 1)
                passed()
                sp.dma_start(m_scr[t].rearrange("b h c -> (b h) c"), key_bias[:]).then_inc(bias_stored, 16)
                sp.wait_ge(bias_stored, (t + 1) * 16)
                passed()
                sp.dma_start(bias_rows[:], m_scr[t].rearrange("b (r g) c -> (b r) (g c)", r=2)).then_inc(bias_ld, 16)

            def tail(it, f, half, chunks=range(KC)):
                for n in chunks:
                    evacuated(sp, it, f"h{n}")
                    passed()
                    sp.dma_start(h_scr[f, :, n, :, half * TOK:(half + 1) * TOK], h_out[:, n % 2].bitcast(F32)).then_inc(h_stored[n % 2], 16)

            def iteration(it, f, par, more_x=True):
                t = it
                if more_x:
                    sp.wait_ge(residual_ready, t + 1)
                    passed()
                    sp.dma_start(x_in[:, par], x_v[t + 2]).then_inc(x_ld[par], 16)
                last = isinstance(it, int) and it == NT - 1
                if f is not None:
                    tail(it, f, 1 - par, (0, 1))
                if not last:
                    route(it, t + 1)
                if f is not None:
                    tail(it, f, 1 - par, (2, 3))
                if not last:
                    bias(t + 1)
                evacuated(sp, it, "o0")
                passed()
                evacuated(sp, it, "o1")
                passed()
                sp.dma_start(x1_v[t], x1[:]).then_inc(x1_stored, 16)

            def load_slot(g, k):
                sp.dma_start(w_slot[k][:].bitcast(F32), w_scr[g * GB + k]).then_inc(slot_ld[k], 16)

            def load_tile(s, par):
                sp.dma_start(h_in[par][:].bitcast(F32), h_scr[s]).then_inc(h_ld[par], 16)

            route(AHEAD, 0)
            load_raw(SPLIT["wo"] - 1)
            load_raw(SPLIT["w2"] - 1)
            bias(0)
            iteration(0, None, 0)
            with sp.Fori(0, NT // 2 - 2) as n:
                iteration(n * 2 + 1, n, 1)
                iteration(n * 2 + 2, n, 0)
            iteration(NT - 3, NF - 2, 1)
            iteration(NT - 2, NF - 2, 0, more_x=False)

            evacuated(sp, NT - 2, "q3")
            for q in w_stored:
                sp.wait_ge(q, 48)
            load_slot(0, 0)
            sp.wait_ge(scores_full, NT * NP)
            for q in h_stored:
                sp.wait_ge(q, KC * 16 + PRIMED)
            load_tile(0, 0)
            iteration(NT - 1, NF - 1, 1, more_x=False)
            tail(BEHIND, NF - 1, 1)
            for q in w_stored:
                sp.wait_ge(q, 2 * 48)
            load_slot(0, 1)

            for q in h_stored:
                sp.wait_ge(q, NT * (KC // 2) * 16 + PRIMED)
            sp.wait_ge(x1_stored, NT * 16 + PRIMED)

            def load_acc(s, par):
                sp.dma_start(acc[par][:], out_tiles[s]).then_inc(acc_ld[par], 16)

            for q in w_stored:
                sp.wait_ge(q, GB * 48)
            for k in range(2, GB):
                load_slot(0, k)
            load_tile(1, 1)
            load_acc(0, 0)
            load_acc(1, 1)

            def store(i, s, par):
                sp.wait_ge(acc_added, (i + 1) * NQ)
                passed()
                sp.dma_start(out_tiles[s], acc[par][:]).then_inc(acc_stored[par], 16)

            def step(pair, i, s_before, s_next):
                sp.wait_ge(down_done, i * (NS - 1) - 1)
                passed()
                load_tile(s_next, 1)
                store(i - 1, s_before, 1)
                sp.wait_ge(acc_stored[1], pair * 16)
                passed()
                load_acc(s_next, 1)

            NPAIR = NF // 2

            def pair_body(g, p, first=False, last_of_group=False, very_last=False):
                pair = g * NPAIR + p
                i0 = pair * 2
                s0 = p * 2
                wrap_before = (NF - 1) if (isinstance(p, int) and p == 0) else s0 - 1
                if not first:
                    step(pair, i0, wrap_before, s0 + 1)
                i1 = i0 + 1
                s_next = 0 if last_of_group else s0 + 2
                if very_last:
                    store(i1 - 1, s0, 0)
                    return
                sp.wait_ge(down_done, i1 * (NS - 1) - 1)
                passed()
                load_tile(s_next, 0)
                if last_of_group:
                    weights_stored((g + 2) * GB)
                    for k in range(GB):
                        if k == GB - 1:
                            store(i1 - 1, s0, 0)
                        if k < GB - 1:
                            sp.wait_ge(down_done, i1 * (NS - 1) + 2 * k + 2)
                        else:
                            sp.wait_ge(down_full, (i1 + 1) * NQ)
                        passed()
                        load_slot(g + 1, k)
                else:
                    store(i1 - 1, s0, 0)
                sp.wait_ge(acc_stored[0], (pair + 1) * 16)
                passed()
                load_acc(s_next, 0)

            def weights_stored(blocks):
                for q in w_stored:
                    sp.wait_ge(q, blocks * 48)
                    passed()

            def group(g, last_group):
                if isinstance(g, int) and g == 0:
                    pair_body(0, 0, first=True)
                else:
                    pair_body(g, 0)
                if NPAIR > 2:
                    with sp.Fori(1, NPAIR - 1) as p:
                        pair_body(g, p)
                pair_body(g, NPAIR - 1, last_of_group=True, very_last=last_group)

            group(0, NG == 1)
            if NG > 2:
                with sp.Fori(1, NG - 1) as g:
                    group(g, False)
            group(NG - 1, True)
            i_last = NG * NF - 1
            sp.wait_ge(acc_added, (i_last + 1) * NQ)
            sp.dma_start(out_tiles[NF - 1], acc[1][:]).then_inc(acc_stored[1], 16)
            sp.wait_ge(acc_stored[0], NG * NPAIR * 16)
            sp.wait_ge(acc_stored[1], NG * NPAIR * 16)

        @block.gpsimd
        def _(pool):
            pool.sem_inc(w_step, PRIMED)

            def passed():
                pool.sem_inc(pool_passed, 1)

            def load_packed(c, m):
                name = ("gate", "up", "down")[m]
                pool.dma_start(packed[:, m, :], a[name + "_packed"][c]).then_inc(packed_ld[m], 16)
                if m < 2:
                    for k in range(2):
                        pool.dma_start(scales[:, m, k * 256:(k + 1) * 256],
                                       a[name + "_scales"][c, 8 * k:8 * k + 8, :].unsqueeze(1).to_broadcast([8, 16, 256])).then_inc(packed_ld[m], 16)
                else:
                    pool.dma_start(scales[:, m, :], a[name + "_scales"][c].unsqueeze(1).to_broadcast([8, 16, 512])).then_inc(packed_ld[m], 16)

            pool.wait_ge(cond_row_ready, 1)

            def gather(pairs):
                for q in pairs:
                    pool.indirect_dma_start(mix[:, q, :], None, cond_rows, bass.IndirectOffsetOnAxis(ap=cond_row[:, q:q + 1], axis=0)) \
                        .then_inc(gather_first if q < NP else gather_second if q < 2 * NP else gather_rest, 16)

            gather(range(2 * NP))
            load_packed(0, 0)
            pool.memset(k_diagonal[:].bitcast(F32), 0.0).then_inc(k_cleared, 1)

            def weight_block(c, k, last):
                m, nib = k // 2, k % 2
                par = k % 2
                pool.wait_ge(dq_step, c * 36 + 6 * k + 6)
                pool.tensor_tensor(lut_v[:, par, :], lut_v[:, par, :], signed_scale[:, par, :].bitcast(F32), ALU.mult).then_inc(w_used, 1)
                if nib == 1 and not last:
                    load_packed(c + 1, m)
                if k >= 2:
                    pool.wait_ge(w_stored[par], (c * 3 + m) * 16)
                    passed()
                pool.wait_ge(w_used, c * 6 + k + 1)
                passed()
                pool.tensor_copy(w_parts[:, par, HI, :], lut_v[:, par, :]).then_inc(w_step, 1)
                pool.wait_ge(w_step, c * 12 + 2 * k + 1 + PRIMED)
                pool.tensor_tensor(w_parts[:, par, LO, :], lut_v[:, par, :], w_parts[:, par, HI, :].bitcast(F32), ALU.subtract).then_inc(w_step, 1)
                pool.wait_ge(w_step, c * 12 + 2 * k + 2 + PRIMED)
                passed()
                pool.dma_start(w_scr[c, :, m, nib], w_parts[:, par].bitcast(F32)).then_inc(w_stored[par], 16)
                if k == 5:
                    for q in w_stored:
                        pool.wait_ge(q, (c + 1) * 48)
                        passed()

            def k_low(t):
                pool.wait_ge(k_hi, t + 1)
                pool.tensor_tensor(rope_in[:, 0], rope_in[:, 0], k_whole[:].bitcast(F32), ALU.subtract).then_inc(k_lo, 1)

            def q_low(t):
                pool.wait_ge(q_hi, t * 2 + 1)
                pool.tensor_tensor(q_parts[:, LO, 0].rearrange("p b r c -> p r b c"), rope_in[:, 1].rearrange("p r (b c) -> p r b c", c=C),
                                   q_parts[:, HI, 0].rearrange("p b r c -> p r b c").bitcast(F32), ALU.subtract).then_inc(q_ready[0], 1)

            def iteration(t, par, c, k0, do_head=True):
                pool.wait_ge(x1_stored, t * 16 + PRIMED)
                passed()
                pool.wait_ge(turn_used, t * NP + PRIMED)
                passed()
                for q in range(NP):
                    ins = pool.tensor_tensor(x1[:, q, :], x_in[:, par, q, :], bo[:], ALU.add)
                ins.then_inc(residual_ready, 1)
                weight_block(c, k0, False)
                if do_head:
                    k_low(t + 1)
                weight_block(c, k0 + 1, False)
                if do_head:
                    q_low(t + 1)
                weight_block(c, k0 + 2, False)

            pool.wait_ge(const_ld, N_CONST * 16)
            pool.wait_ge(x_ld[0], 16)
            gather(range(2 * NP, B // 4))
            k_low(0)
            gather(range(B // 4, B // 4 + 2))
            q_low(0)
            gather(range(B // 4 + 2, B // 2))
            load_packed(0, 1)
            load_packed(0, 2)
            iteration(0, 0, 0, 0)
            with pool.Fori(0, NT // 2 - 1) as n:
                iteration(n * 2 + 1, 1, n, 3)
                iteration(n * 2 + 2, 0, n + 1, 0)
            iteration(NT - 1, 1, NT // 2 - 1, 3, do_head=False)
            with pool.Fori(NF, NCP - 1) as c:
                for k in range(6):
                    weight_block(c, k, False)
            for k in range(6):
                weight_block(NCP - 1, k, True)
            for q in w_stored:
                pool.wait_ge(q, NCP * 48)

        @block.tensor
        def _(pe):
            def passed():
                pe.sem_inc(pe_passed, 1)

            def ready(it, name):
                pe.wait_ge(proj_free[BANK[name]], uses_before(it, name) + PRIMED)
                return proj[BANK[name]], proj_full[BANK[name]]

            def products(out_ap, pairs, start=True, stop=True):
                for n, (lhsT, rhs) in enumerate(pairs):
                    ins = pe.matmul(out_ap, lhsT, rhs, start=(start and n == 0), stop=(stop and n == len(pairs) - 1))
                return ins

            def mixing(it, t, tt, par, chunks):
                pe.wait_ge(x_ld[par], (tt + 1) * 16)
                pe.wait_ge(mix_ready, t * 2 + 2)
                for c in chunks:
                    bank, done = ready(it, f"hs{c}")
                    for q in range(NP):
                        ins = pe.matmul(bank[:, q * P:(q + 1) * P], x_in[:, par, q, c * P:(c + 1) * P],
                                        mix_tile[:, par, q].rearrange("p b c -> p (b c)"), start=True, stop=True)
                    ins.then_inc(done, 1)

            def routing(it):
                bank, done = ready(it, "z")
                evacuated(pe, it, "hs2")
                evacuated(pe, it, "hs3")
                products(bank[0:HEADS, 0:TOK], [(wr[:, i, c, :], hs[:, j, c, :]) for c in range(KC) for i, j in THREE]).then_inc(done, 1)

            def project(it, name, w):
                bank, done = ready(it, name)
                n = int(name[1])
                products(bank[:, 0:TOK], [(w[:, i, c, n * P:(n + 1) * P], hs[:, j, c, :]) for c in range(KC) for i, j in THREE]).then_inc(done, 1)

            def value(it, q):
                bank, done = ready(it, f"v{q}")
                products(bank[:, 0:256], [(hs[:, i, c, q * P:(q + 1) * P], wv[:, j, c, :]) for c in range(KC) for i, j in THREE]).then_inc(done, 1)

            def score(t, q):
                if not (isinstance(t, int) and t == 0):
                    pe.wait_ge(pT_used, (t - 1) * NP + q + 1)
                for b in range(2):
                    pe.matmul(scores[q][:, b].rearrange("p g c -> p (g c)"), batch_rows[:, 2 * q + b, :], bias_rows[:],
                              start=True, stop=False, skip_group_check=True)
                for b in range(2):
                    for gc in range(2):
                        for i, j in THREE:
                            ins = pe.matmul(scores[q][:, b, 4 * gc:4 * gc + 4, :].rearrange("p g c -> p (g c)"),
                                            q_parts[:, i, gc, 2 * q + b].rearrange("p r c -> p (r c)"),
                                            k_diagonal[:, j, 2 * q + b, gc].rearrange("p g c -> p (g c)"),
                                            start=False, stop=(gc == 1 and (i, j) == THREE[-1]), skip_group_check=True)
                ins.then_inc(scores_full, 1)

            def turn_probs(t, q):
                pe.wait_ge(probs_ready, t * NP + q + 1)
                for g in range(KV_HEADS):
                    ins = pe.transpose(pT[q][:, g, :], probs[:, q, g].rearrange("p b c -> p (b c)"), identity[:])
                ins.then_inc(pT_full, 1)

            def attend(it, t, q):
                pe.wait_ge(pT_used, t * NP + q + 1)
                pe.wait_ge(pv_used, t * NP + q + PRIMED)
                evacuated(pe, it, f"v{q}")
                passed()
                for b in range(2):
                    if b == 1:
                        pe.wait_ge(pv_step, t * NP + q + 1)
                        passed()
                    rows = slice(b * C, (b + 1) * C)
                    for g in range(KV_HEADS):
                        gc, i = g // 4, g % 4
                        ins = pe.matmul(pv[32 * i:32 * i + 32, gc, :, b, :], v_sb[rows, q, g, :], probsT[rows, g, :],
                                        start=True, stop=True, tile_position=(b * C, 32 * i))
                    ins.then_inc(pv_step if b == 0 else pv_full, 1)

            def turn_rows(it, t, q):
                evacuated(pe, it, f"o{q}")
                pe.wait_ge(turn_used, t * NP + q + PRIMED)
                for c in range(KC):
                    ins = pe.transpose(turn[:, c, :], x1[:, q, c * P:(c + 1) * P], identity[:])
                ins.then_inc(turn_full, 1)

            def out_proj(it, t, q):
                bank, done = ready(it, f"o{q}")
                pe.wait_ge(pv_used, t * NP + q + 1 + PRIMED)
                products(bank[:], [(attnT[:, i, c, :], wo[:, j, c, :]) for c in range(KC) for i, j in THREE]).then_inc(done, 1)

            def adapter_ranks(it, t):
                bank, done = ready(it, "xa")
                pe.wait_ge(turn_used, (t + 1) * NP + PRIMED)
                products(bank[:, 0:TOK], [(wa[:, i, c, :], x1T[:, j, c, :]) for c in range(KC) for i, j in THREE]).then_inc(done, 1)

            def hidden_main(it, n):
                bank, done = ready(it, f"h{n}")
                products(bank[:, 0:TOK], [(w2[:, i, c, n * P:(n + 1) * P], x1T[:, j, c, :]) for c in range(KC) for i, j in THREE], stop=False)

            def hidden_adapter(n):
                products(proj[BANK[f"h{n}"]][:, 0:TOK], [(wb[:, i, n * P:(n + 1) * P], xa_parts[:, j, :]) for i, j in THREE],
                         start=False).then_inc(proj_full[BANK[f"h{n}"]], 1)

            def hidden_first(it, t):
                hidden_main(it, 0)
                hidden_main(it, 1)
                pe.wait_ge(xa_lo, t + 1)
                hidden_adapter(0)
                hidden_adapter(1)

            def hidden_rest(it):
                for n in (2, 3):
                    hidden_main(it, n)
                    hidden_adapter(n)

            def iteration(t, par, tt_next, do_tail=True, do_head=True):
                it = t
                if not do_tail:
                    pe.wait_ge(raw_lo, SPLIT["wv"])
                value(it, 0)
                value(it, 1)
                pe.wait_ge(bias_ld, (t + 1) * 16)
                pe.wait_ge(k_ready, t + 1)
                for half in q_ready:
                    pe.wait_ge(half, t + 1)
                score(t, 0)
                if do_tail:
                    adapter_ranks(it, t - 1)
                score(t, 1)
                if do_tail:
                    hidden_first(it, t - 1)
                turn_probs(t, 0)
                if do_head:
                    mixing(it, t + 1, tt_next, 1 - par, (0, 1))
                attend(it, t, 0)
                if do_head:
                    mixing(it, t + 1, tt_next, 1 - par, (2, 3))
                    routing(it)
                    project(it, "k0", wk)
                    project(it, "k1", wk)
                turn_probs(t, 1)
                if do_tail:
                    hidden_rest(it)
                if not do_tail:
                    pe.wait_ge(raw_lo, SPLIT["wo"])
                out_proj(it, t, 0)
                attend(it, t, 1)
                if do_head:
                    for n in range(4):
                        project(it, f"q{n}", wq)
                turn_rows(it, t, 0)
                out_proj(it, t, 1)
                turn_rows(it, t, 1)

            mixing(AHEAD, 0, 0, 0, range(KC))
            pe.wait_ge(const_made, 1)
            pe.wait_ge(raw_lo, SPLIT["wr"])
            routing(AHEAD)
            pe.wait_ge(raw_lo, SPLIT["wk"])
            for name in ("k0", "k1"):
                project(AHEAD, name, wk)
            pe.wait_ge(raw_lo, SPLIT["wq"])
            for name in ("q0", "q1", "q2", "q3"):
                project(AHEAD, name, wq)
            iteration(0, 0, 0, do_tail=False)
            pe.wait_ge(raw_lo, len(RAW))
            with pe.Fori(0, NT // 2 - 1) as n:
                iteration(n * 2 + 1, 1, n + 1)
                iteration(n * 2 + 2, 0, n + 1)
            iteration(NT - 1, 1, 0, do_head=False)
            adapter_ranks(BEHIND, NT - 1)
            hidden_first(BEHIND, NT - 1)
            hidden_rest(BEHIND)

            for name in ("h2", "h3"):
                evacuated(pe, BEHIND, name)

            def gate_up(i, g, pair, j, par, first):
                k, nib_n = j // 2, j % 2
                if j == 0:
                    pe.wait_ge(h_ld[par], (pair + 1) * 16)
                if j % 2 == 0:
                    pe.wait_ge(slot_ld[k], (g + 1) * 16)
                if j >= 2 or not first:
                    pe.wait_ge(inter_done, i * NS + j - 1)
                for m, bank, done in ((0, gate, gate_full), (1, up, up_full)):
                    pairs = [(w_slot[k][:, m, nib, u, c * 256 + nib_n * P:c * 256 + (nib_n + 1) * P], h_in[par][:, 2 * c + nib, v, :])
                             for c in range(2) for nib in range(2) for u, v in THREE]
                    products(bank[j % 2][:], pairs).then_inc(done[j % 2], 1)

            def down_step(i, j, first=False):
                k, nib_n = j // 2, j % 2
                pe.wait_ge(inter_ready, i * NS + j + 1)
                for tc in range(NQ):
                    if j == 0 and not first:
                        pe.wait_ge(acc_added, (i - 1) * NQ + tc + 1)
                    for m, (u, v) in enumerate(THREE):
                        ins = pe.matmul(down[tc][:], inter_parts[:, j % 2, u, tc * P:(tc + 1) * P], w_slot[k][:, 2, nib_n, v, :],
                                        start=(j == 0 and m == 0), stop=(j == NS - 1 and m == 2))
                    if j == NS - 1:
                        ins.then_inc(down_full, 1)
                if j < NS - 1:
                    ins.then_inc(down_done, 1)

            def ffn_tile(g, pair, par, first=False):
                i = pair * 2 + par
                for j in range(NS):
                    gate_up(i, g, pair, j, par, first)
                    if j >= 2:
                        down_step(i, j - 2, first)
                    elif not first:
                        down_step(i - 1, NS - 2 + j)

            NPAIR = NF // 2
            ffn_tile(0, 0, 0, first=True)
            ffn_tile(0, 0, 1)
            with pe.Fori(1, NPAIR) as p:
                ffn_tile(0, p, 0)
                ffn_tile(0, p, 1)
            with pe.Fori(1, NG) as g:
                with pe.Fori(0, NPAIR) as p:
                    ffn_tile(g, g * NPAIR + p, 0)
                    ffn_tile(g, g * NPAIR + p, 1)
            for j in (NS - 2, NS - 1):
                down_step(NG * NF - 1, j)

        @block.scalar
        def _(act):
            def split(j):
                stage, hi, lo = raw_views(j)
                act.wait_ge(raw_ld[RAW[j][3]], (len(stage_uses(j)) + 1) * 16)
                act.activation(hi, stage, ACT.Copy).then_inc(raw_hi, 1)

            def mix_diagonal(t, par):
                for b in range(2):
                    rows = slice(b * C, (b + 1) * C)
                    act.activation(mix_tile[rows, par, :, b, :], mix[rows, bass.ds(t * NP, NP), :], ACT.Copy).then_inc(mix_ready, 1)

            def mixed(it, chunks):
                for c in chunks:
                    bank = full_wait(act, it, f"hs{c}")
                    act.activation(hs[:, HI, c, :], bank[:, 0:TOK], ACT.Copy).then_inc(hs_hi, 1)

            def logits(it):
                bank = full_wait(act, it, "z")
                act.activation(z_sb, bank[0:HEADS, 0:TOK], ACT.Identity, bias=br[:, 0:1]).then_inc(proj_free[BANK["z"]], 1)

            def rope_bias(it, t, c):
                name = ROPE[c]
                bank = full_wait(act, it, name)
                bias = bk[:, c:c + 1] if c < 2 else bq[:, c - 2:c - 1]
                if c >= 4:
                    act.wait_ge(k_ready, t + 1)
                act.activation(rope_in[:, c // 2 % 2, c % 2, :], bank[:, 0:TOK], ACT.Identity, bias=bias).then_inc(proj_free[BANK[name]], 1)

            def k_high(t):
                act.wait_ge(rope_done, t * 3 + 1)
                act.activation(k_whole[:], rope_in[:, 0], ACT.Copy).then_inc(k_hi, 1)

            def k_place(t):
                act.wait_ge(k_hi, t + 1)
                for part, src in ((HI, k_whole), (LO, rope_in[:, 0])):
                    if part == LO:
                        act.wait_ge(k_lo, t + 1)
                    for i in range(4):
                        rows = slice(32 * i, 32 * i + 32)
                        ins = act.activation(k_diagonal[rows, part, :, :, i, :], src[rows].rearrange("p k (b c) -> p b k c", c=C), ACT.Copy)
                ins.then_inc(k_ready, 1)

            def q_high(t, gc):
                act.wait_ge(rope_done, t * 3 + gc + 2)
                act.activation(q_parts[:, HI, gc].rearrange("p b r c -> p r b c"), rope_in[:, 1 - gc].rearrange("p r (b c) -> p r b c", c=C),
                               ACT.Copy).then_inc(q_hi, 1)

            def exp(t, q):
                act.wait_ge(scores_used, t * NP + q + 1)
                act.activation(probs[:, q], probs[:, q], ACT.Exp, scale=ATT_SCALE).then_inc(exp_done, 1)

            def probs_turned(t, q):
                act.wait_ge(pT_full, t * NP + q + 1)
                act.activation(probsT[:], pT[q], ACT.Copy).then_inc(pT_used, 1)

            def heads_high(t, q):
                act.wait_ge(pv_full, t * NP + q + 1)
                act.activation(attnT[:, HI].rearrange("p k n -> p (k n)"), pv[:].rearrange("p g r b c -> p (g r b c)"), ACT.Copy).then_inc(pv_hi, 1)

            def rows_high(t, q):
                act.wait_ge(turn_full, t * NP + q + 1)
                act.activation(x1T[:, HI, :, q * P:(q + 1) * P], turn[:], ACT.Copy).then_inc(turn_hi, 1)

            def ranks(it):
                evacuated(act, it, "xa")
                act.activation(xa_parts[:, HI, :], xa[:], ACT.Copy).then_inc(xa_hi, 1)

            def hidden(it, t, n):
                bank = full_wait(act, it, f"h{n}")
                act.wait_ge(h_stored[n % 2], (t * (KC // 2) + n // 2) * 16 + PRIMED)
                act.activation(h_out[:, n % 2, HI, :], bank[:, 0:TOK], ACT.Copy).then_inc(h_hi, 1)

            def iteration(t, par, do_tail=True, do_head=True):
                it = t
                if do_head:
                    mix_diagonal(t + 1, 1 - par)
                exp(t, 0)
                if do_tail:
                    ranks(it)
                    hidden(it, t - 1, 0)
                    hidden(it, t - 1, 1)
                probs_turned(t, 0)
                if do_head:
                    mixed(it, (0, 1))
                exp(t, 1)
                if do_head:
                    mixed(it, (2, 3))
                heads_high(t, 0)
                if do_head:
                    logits(it)
                    rope_bias(it, t + 1, 0)
                    rope_bias(it, t + 1, 1)
                probs_turned(t, 1)
                if do_tail:
                    hidden(it, t - 1, 2)
                if do_head:
                    k_high(t + 1)
                if do_tail:
                    hidden(it, t - 1, 3)
                if do_head:
                    k_place(t + 1)
                heads_high(t, 1)
                if do_head:
                    for n in (2, 3, 4, 5):
                        rope_bias(it, t + 1, n)
                rows_high(t, 0)
                if do_head:
                    q_high(t + 1, 0)
                    q_high(t + 1, 1)
                rows_high(t, 1)

            split(0)
            split(1)
            act.wait_ge(mix_cleared, 1)
            act.wait_ge(gather_first, NP * 16)
            mix_diagonal(0, 0)
            split(2)
            split(3)
            mixed(AHEAD, range(KC))
            act.wait_ge(const_ld, N_CONST * 16)
            logits(AHEAD)
            split(4)
            rope_bias(AHEAD, 0, 0)
            rope_bias(AHEAD, 0, 1)
            split(5)
            act.wait_ge(k_cleared, 1)
            k_high(0)
            rope_bias(AHEAD, 0, 2)
            rope_bias(AHEAD, 0, 3)
            k_place(0)
            q_high(0, 0)
            rope_bias(AHEAD, 0, 4)
            rope_bias(AHEAD, 0, 5)
            split(6)
            q_high(0, 1)
            split(7)
            act.wait_ge(gather_second, NP * 16)
            iteration(0, 0, do_tail=False)
            act.wait_ge(gather_rest, (B // 2 - 2 * NP) * 16)
            with act.Fori(0, NT // 2 - 1) as n:
                iteration(n * 2 + 1, 1)
                iteration(n * 2 + 2, 0)
            iteration(NT - 1, 1, do_head=False)
            ranks(BEHIND)
            for n in range(KC):
                hidden(BEHIND, NT - 1, n)

            def ffn_tile(i, first=False):
                for j in range(NS):
                    b = j % 2
                    n = i * (NS // 2) + j // 2
                    act.wait_ge(gate_full[b], n + 1)
                    act.activation(gate_sq[:], gate[b][:], ACT.Square).then_inc(sq_done, 1)
                    act.wait_ge(gin_done, i * NS + j + 1)
                    act.activation(gate_tanh[:], gate_in[:], ACT.Tanh, scale=GELU_SCALE * GELU_CUBIC).then_inc(tanh_done, 1)
                    if not (first and j < 2):
                        if j == 1:
                            act.wait_ge(down_full, i * NQ)
                        else:
                            act.wait_ge(down_done, i * (NS - 1) + max(j - 1, 0))
                    act.wait_ge(inter_done, i * NS + j + 1)
                    act.activation(inter_parts[:, b, HI, :], inter[:], ACT.Copy).then_inc(inter_hi, 1)

            ffn_tile(0, first=True)
            with act.Fori(1, NG * NF) as i:
                ffn_tile(i)

        @block.vector
        def _(dve):
            for q in (*proj_free, pv_used, turn_used):
                dve.sem_inc(q, PRIMED)

            def passed():
                dve.sem_inc(dve_passed, 1)

            dve.wait_ge(index_ld, 48)
            dve.tensor_scalar(cond_row[:], cond_of[:], float(C), columns[:, 0:1], ALU.mult, ALU.add).then_inc(cond_row_ready, 1)
            dve.memset(mix_tile[:], 0.0).then_inc(mix_cleared, 1)

            def dequantise(c, k, halves=(0, 1)):
                m, nib = k // 2, k % 2
                base = c * 36 + 6 * k
                sign = signed_scale[:, k % 2, :]
                if 0 in halves:
                    if nib == 0:
                        dve.wait_ge(packed_ld[m], (c + 1) * (48 if m < 2 else 32))
                    if not (isinstance(c, int) and c == 0 and k == 0):
                        dve.wait_ge(dq_step, base)
                    if k >= 2 or not (isinstance(c, int) and c == 0):
                        dve.wait_ge(w_step, c * 12 + 2 * k - 2 + PRIMED)
                    dve.tensor_scalar(magnitude[:], packed[:, m, :], 4 * nib, 7, ALU.logical_shift_right, ALU.bitwise_and).then_inc(dq_step, 1)
                    dve.tensor_scalar(sign, packed[:, m, :], 28 - 4 * nib, -2 ** 31, ALU.logical_shift_left, ALU.bitwise_and).then_inc(dq_step, 1)
                    dve.wait_ge(dq_step, base + 1)
                    dve.tensor_scalar(lut_line[:], magnitude[:], 2.0, -8.0, ALU.mult, ALU.add).then_inc(dq_step, 1)
                    dve.wait_ge(dq_step, base + 2)
                    dve.tensor_tensor(sign, sign, scales[:, m, :].bitcast(I32), ALU.bitwise_xor).then_inc(dq_step, 1)
                if 1 in halves:
                    dve.wait_ge(dq_step, base + 3)
                    dve.scalar_tensor_tensor(lut_line[:], magnitude[:], -2.0, lut_line[:], ALU.add, ALU.max).then_inc(dq_step, 1)
                    dve.wait_ge(dq_step, base + 5)
                    dve.scalar_tensor_tensor(lut_v[:, k % 2, :], magnitude[:], 0.5, lut_line[:], ALU.mult, ALU.max).then_inc(dq_step, 1)

            def split(j):
                stage, hi, lo = raw_views(j)
                dve.wait_ge(raw_hi, j + 1)
                dve.tensor_tensor(lo, stage, hi.bitcast(F32), ALU.subtract).then_inc(raw_lo, 1)

            def mixed(t, chunks):
                for c in chunks:
                    name = f"hs{c}"
                    dve.wait_ge(hs_hi, t * KC + c + 1)
                    dve.tensor_tensor(hs[:, LO, c, :], proj[BANK[name]][:, 0:TOK], hs[:, HI, c, :].bitcast(F32), ALU.subtract) \
                       .then_inc(proj_free[BANK[name]], 1)

            def rope(it, t, n):
                values = rope_in[:, n % 2]

                def by_position(buf):
                    return buf.rearrange("p k (b c) -> p (k b) c", c=C)

                s0 = (t * 3 + n) * 3
                if not (isinstance(t, int) and t == 0 and n == 0):
                    dve.wait_ge(rope_done, t * 3 + n)
                    passed()
                for c in (2 * n, 2 * n + 1):
                    evacuated(dve, it, ROPE[c])
                    passed()
                dve.stream_shuffle(rope_sin[:], values, [(i + HD // 2) % HD for i in range(HD)]).then_inc(rope_step, 1)
                dve.wait_ge(rope_step, s0 + 1)
                dve.tensor_tensor(by_position(values), by_position(values), cos[:].unsqueeze(1).to_broadcast([P, 2 * NB, C]), ALU.mult).then_inc(rope_step, 1)
                dve.tensor_tensor(by_position(rope_sin[:]), by_position(rope_sin[:]), sin[:].unsqueeze(1).to_broadcast([P, 2 * NB, C]), ALU.mult).then_inc(rope_step, 1)
                dve.wait_ge(rope_step, s0 + 3)
                dve.tensor_tensor(values, values, rope_sin[:], ALU.add).then_inc(rope_done, 1)

            def q_low(t):
                dve.wait_ge(q_hi, t * 2 + 2)
                dve.tensor_tensor(q_parts[:, LO, 1].rearrange("p b r c -> p r b c"), rope_in[:, 0].rearrange("p r (b c) -> p r b c", c=C),
                                  q_parts[:, HI, 1].rearrange("p b r c -> p r b c").bitcast(F32), ALU.subtract).then_inc(q_ready[1], 1)

            def top_keys(t):
                steps = 2 * TOPK // 8 + 1
                s0 = t * steps
                dve.wait_ge(z_ld, (t + 1) * 16)
                dve.tensor_scalar(rank[:], z_rows[:], SIGMOID_ONE, SIGMOID_ZERO, ALU.min, ALU.max).then_inc(topk_step, 1)
                for r in range(TOPK // 8):
                    dve.wait_ge(topk_step, s0 + 2 * r + 1)
                    passed()
                    dve.max(top8[:], rank[:]).then_inc(topk_step, 1)
                    dve.wait_ge(topk_step, s0 + 2 * r + 2)
                    passed()
                    dve.match_replace(rank[:], top8[:], rank[:], PICKED).then_inc(topk_step, 1)
                dve.wait_ge(topk_step, s0 + steps)
                dve.tensor_scalar(key_bias[:], rank[:], PICKED / 2, MASKED, ALU.is_gt, ALU.mult).then_inc(bias_ready, 1)

            def value(it, q):
                bank = full_wait(dve, it, f"v{q}")
                dve.tensor_tensor(v_sb[:, q].rearrange("p g d -> p (g d)"), bank[:, 0:256], bv[:], ALU.add).then_inc(proj_free[BANK[f"v{q}"]], 1)

            def softmax_shift(t, q):
                dve.wait_ge(scores_full, t * NP + q + 1)
                dve.tensor_reduce(row_max[:, q], scores[q][:], AX_X, ALU.max).then_inc(scores_max, 1)
                dve.wait_ge(scores_max, t * NP + q + 1)
                dve.tensor_tensor(probs[:, q].rearrange("p g b c -> p b g c"), scores[q][:],
                                  row_max[:, q].unsqueeze(3).to_broadcast([P, 2, KV_HEADS, C]), ALU.subtract).then_inc(scores_used, 1)

            def softmax_sum(t, q):
                dve.wait_ge(exp_done, t * NP + q + 1)
                dve.tensor_reduce(row_sum[:, q], probs[:, q].rearrange("p g b c -> p b g c"), AX_X, ALU.add).then_inc(sum_step, 1)
                dve.wait_ge(sum_step, (t * NP + q) * 2 + 1)
                dve.reciprocal(row_inv[:, q], row_sum[:, q]).then_inc(sum_step, 1)

            def normalise(t, q):
                dve.wait_ge(sum_step, (t * NP + q) * 2 + 2)
                pr = probs[:, q].rearrange("p g b c -> p b g c")
                dve.tensor_tensor(pr, pr, row_inv[:, q].unsqueeze(3).to_broadcast([P, 2, KV_HEADS, C]), ALU.mult).then_inc(probs_ready, 1)

            def heads_low(t, q):
                dve.wait_ge(pv_hi, t * NP + q + 1)
                dve.tensor_tensor(attnT[:, LO].rearrange("p k n -> p (k n)"), pv[:].rearrange("p g r b c -> p (g r b c)"),
                                  attnT[:, HI].rearrange("p k n -> p (k n)").bitcast(F32), ALU.subtract).then_inc(pv_used, 1)

            def rows_low(t, q):
                dve.wait_ge(turn_hi, t * NP + q + 1)
                hi, lo = (x1T[:, u, :, q * P:(q + 1) * P] for u in (HI, LO))
                dve.tensor_tensor(lo, turn[:], hi.bitcast(F32), ALU.subtract).then_inc(turn_used, 1)

            def add_residual(it, t, q):
                bank = full_wait(dve, it, f"o{q}")
                if q == 0:
                    dve.wait_ge(residual_ready, t + 1)
                dve.tensor_tensor(x1[:, q, :], bank[:], x1[:, q, :], ALU.add).then_inc(proj_free[BANK[f"o{q}"]], 1)

            def mask_ranks(it, t):
                bank = full_wait(dve, it, "xa")
                dve.tensor_tensor(xa[:].rearrange("p (b c) -> p b c", c=C), bank[:, 0:TOK].rearrange("p (b c) -> p b c", c=C),
                                  adapter_mask[:, bass.ds(t * NB, NB)].unsqueeze(2).to_broadcast([P, NB, C]), ALU.mult).then_inc(proj_free[BANK["xa"]], 1)

            def ranks_low(t):
                dve.wait_ge(xa_hi, t + 1)
                dve.tensor_tensor(xa_parts[:, LO, :], xa[:], xa_parts[:, HI, :].bitcast(F32), ALU.subtract).then_inc(xa_lo, 1)

            def hidden(t, n):
                dve.wait_ge(h_hi, t * KC + n + 1)
                dve.tensor_tensor(h_out[:, n % 2, LO, :], proj[BANK[f"h{n}"]][:, 0:TOK], h_out[:, n % 2, HI, :].bitcast(F32), ALU.subtract) \
                   .then_inc(proj_free[BANK[f"h{n}"]], 1)

            def iteration(t, c, k0, before, do_tail=True, do_head=True):
                it = t
                value(it, 0)
                value(it, 1)
                if before is not None:
                    dequantise(*before, (1,))
                softmax_shift(t, 0)
                dequantise(c, k0, (0,))
                if do_tail:
                    mask_ranks(it, t - 1)
                softmax_sum(t, 0)
                if do_tail:
                    ranks_low(t - 1)
                normalise(t, 0)
                if do_tail:
                    hidden(t - 1, 0)
                    hidden(t - 1, 1)
                softmax_shift(t, 1)
                if do_head:
                    mixed(t + 1, (0, 1))
                dequantise(c, k0, (1,))
                if do_head:
                    mixed(t + 1, (2, 3))
                softmax_sum(t, 1)
                normalise(t, 1)
                heads_low(t, 0)
                dequantise(c, k0 + 1, (0,))
                if do_head:
                    rope(it, t + 1, 0)
                if do_tail:
                    hidden(t - 1, 2)
                    hidden(t - 1, 3)
                dequantise(c, k0 + 1, (1,))
                add_residual(it, t, 0)
                if do_head:
                    top_keys(t + 1)
                heads_low(t, 1)
                dequantise(c, k0 + 2, (0,))
                if do_head:
                    rope(it, t + 1, 1)
                rows_low(t, 0)
                add_residual(it, t, 1)
                if do_head:
                    rope(it, t + 1, 2)
                    q_low(t + 1)
                rows_low(t, 1)

            for j in range(4):
                split(j)
            dve.wait_ge(const_ld, N_CONST * 16)
            dve.tensor_copy(batch_rows[:], batch_rows_f[:])
            dve.tensor_scalar(adapter_mask[:], adapter_of[:], columns[:, 1:2], adapter_scale[:, 0:1],
                              ALU.is_equal, ALU.mult).then_inc(const_made, 1)
            mixed(0, range(KC))
            split(4)
            rope(AHEAD, 0, 0)
            split(5)
            rope(AHEAD, 0, 1)
            top_keys(0)
            rope(AHEAD, 0, 2)
            split(6)
            q_low(0)
            split(7)
            iteration(0, 0, 0, None, do_tail=False)
            with dve.Fori(0, NT // 2 - 1) as n:
                iteration(n * 2 + 1, n, 3, (n, 2))
                iteration(n * 2 + 2, n + 1, 0, (n, 5))
            iteration(NT - 1, NT // 2 - 1, 3, (NT // 2 - 1, 2), do_head=False)
            dequantise(NT // 2 - 1, 5, (1,))
            mask_ranks(BEHIND, NT - 1)
            ranks_low(NT - 1)
            for n in range(KC):
                hidden(NT - 1, n)

            def add_down(i, pair, par):
                dve.wait_ge(acc_ld[par], (pair + 1) * 16)
                for tc in range(NQ):
                    dve.wait_ge(down_full, i * NQ + tc + 1)
                    dve.tensor_tensor(acc[par][:, tc, :], down[tc][:], acc[par][:, tc, :], ALU.add).then_inc(acc_added, 1)

            def ffn_tile(pair, par, first=False, block_c=None):
                i = pair * 2 + par
                for j in range(NS):
                    b = j % 2
                    n = i * NS + j + 1
                    dve.wait_ge(sq_done, n)
                    dve.scalar_tensor_tensor(gate_in[:], gate_sq[:], 1.0 / GELU_CUBIC, gate[b][:], ALU.add, ALU.mult).then_inc(gin_done, 1)
                    if j == 2 and not first:
                        add_down(i - 1, pair - 1 if par == 0 else pair, 1 - par)
                    if block_c is not None and j < 6:
                        dequantise(block_c, j)
                    dve.wait_ge(tanh_done, n)
                    dve.scalar_tensor_tensor(gate_val[:], gate_tanh[:], 1.0, gate[b][:], ALU.add, ALU.mult).then_inc(gval_done, 1)
                    dve.wait_ge(gval_done, n)
                    dve.wait_ge(up_full[b], i * (NS // 2) + j // 2 + 1)
                    dve.scalar_tensor_tensor(inter[:], gate_val[:], 0.5, up[b][:], ALU.mult, ALU.mult).then_inc(inter_done, 1)
                    dve.wait_ge(inter_hi, n)
                    dve.tensor_tensor(inter_parts[:, b, LO, :], inter[:], inter_parts[:, b, HI, :].bitcast(F32), ALU.subtract).then_inc(inter_ready, 1)

            NPAIR = NF // 2
            ffn_tile(0, 0, first=True)
            ffn_tile(0, 1, block_c=NF)
            with dve.Fori(1, NPAIR) as p:
                ffn_tile(p, 0, block_c=p * 2 + NF - 1)
                ffn_tile(p, 1, block_c=p * 2 + NF)
            ffn_tile(NPAIR, 0, block_c=2 * NF - 1)
            ffn_tile(NPAIR, 1)
            with dve.Fori(NPAIR + 1, NG * NPAIR) as p:
                ffn_tile(p, 0)
                ffn_tile(p, 1)
            add_down(NG * NF - 1, NG * NPAIR - 1, 1)


def rope_tables(C):
    inv_freq = (1.0 / ROPE_THETA ** (np.arange(0, HD, 2, dtype=np.float32) / HD)).astype(np.float32)
    freqs = np.arange(C, dtype=np.float32)[:, None] * inv_freq[None, :]
    emb = np.concatenate([freqs, freqs], axis=-1)
    cos, sin = np.cos(emb).astype(np.float32), np.sin(emb).astype(np.float32)
    sin = np.concatenate([-sin[:, :HD // 2], sin[:, HD // 2:]], axis=-1)
    return np.ascontiguousarray(np.tile(cos.T, (4, 1))), np.ascontiguousarray(np.tile(sin.T, (4, 1)))


def kernel(**inputs):
    import numpy as np
    import concourse.bacc as bacc
    from concourse import mybir
    from concourse.bass_utils import run_bass_kernel_spmd

    def get(name):
        return np.asarray(inputs[name])

    x = get("x")
    B, C, D = x.shape
    MLP = get("L0_ffn_gate_W_packed").shape[0]
    NCP = MLP // 256
    NB = TOK // C

    def head_order(w):
        lead = w.shape[:-1]
        w = w.reshape(*lead, 2, 4, 2, HD)
        return np.moveaxis(w, -2, -3).reshape(*lead, HEADS * HD)

    def repeat_major(w):
        return np.swapaxes(w.reshape(*w.shape[:-1], KV_HEADS, 2), -1, -2).reshape(w.shape)

    def nibble_order(w):
        lead = w.shape[:-1]
        return np.swapaxes(w.reshape(*lead, 2, P, 2), -1, -2).reshape(*lead, D)

    def channel_order(w):
        r = w.shape[0]
        return w.reshape(r, NCP, P, 2).transpose(1, 0, 3, 2).reshape(NCP, r, 256)

    def gate_pack(w):
        return channel_order(w.T).reshape(NCP, 2, P, 256).transpose(0, 2, 1, 3).reshape(NCP, P, 512)

    cos, sin = rope_tables(C)
    batch_rows = np.zeros((NB, 2, NB, 2, C), np.float32)
    for b in range(NB):
        for r in range(2):
            batch_rows[b, r, b, r] = 1.0
    batch_rows = batch_rows.reshape(2 * NB, NB, P)
    columns = np.stack([np.arange(P) % C, np.arange(P) // RANK], axis=1).astype(np.float32)
    arrays = {
        "x": x,
        "cond_index": get("itok_B_1_198").reshape(B // 2, 2).T,
        "adapter_index": get("itok_B_0_6")[None, :],
        "cond_weights": get("L0_cond_weights"),
        "wq": head_order(get("L0_attn_Wq")),
        "bq": head_order(get("L0_attn_bq")).reshape(4, P).T,
        "wk": get("L0_attn_Wk"),
        "bk": get("L0_attn_bk").reshape(2, P).T,
        "wv": get("L0_attn_Wv"),
        "bv": get("L0_attn_bv")[None, :],
        "wo": head_order(get("L0_attn_Wo").T).T,
        "bo": get("L0_attn_bo")[None, :],
        "wr": repeat_major(get("L0_attn_Wr")),
        "br": repeat_major(get("L0_attn_br"))[:, None],
        "w2": nibble_order(get("L0_cond2_W").T),
        "wa": get("L0_cond2_A").reshape(ADAPTERS * RANK, D).T,
        "wb": nibble_order(get("L0_cond2_Bm").transpose(0, 2, 1).reshape(ADAPTERS * RANK, D)),
        "adapter_scales": np.repeat(get("L0_cond2_scalings"), RANK)[:, None],
        "gate_packed": gate_pack(get("L0_ffn_gate_W_packed")),
        "gate_scales": channel_order(get("L0_ffn_gate_scales").T),
        "up_packed": gate_pack(get("L0_ffn_up_W_packed")),
        "up_scales": channel_order(get("L0_ffn_up_scales").T),
        "down_packed": get("L0_ffn_down_W_packed").T.reshape(NCP, P, D),
        "down_scales": get("L0_ffn_down_scales").T.reshape(NCP, 8, D),
        "cos": cos, "sin": sin,
        "identity": np.eye(P, dtype=np.float32),
        "batch_rows": batch_rows,
        "columns": columns,
    }
    nc = bacc.Bacc("TRN2", target_bir_lowering=False, num_devices=1)
    given, aps = {}, {}
    for name, v in arrays.items():
        v = np.ascontiguousarray(v)
        given["in_" + name] = v
        aps[name] = nc.dram_tensor("in_" + name, v.shape, mybir.dt.from_np(v.dtype), kind="ExternalInput").ap()
    out = nc.dram_tensor("out_0", (B, C, D), mybir.dt.float32, kind="ExternalOutput").ap()
    build(nc, aps, out)
    r = run_bass_kernel_spmd(nc, [given], core_ids=[0])
    return r.results[0]["out_0"]
```
